# Optimizing a Trainium2 kernel written in Bass

```python
import numpy as np
import jax
import jax.numpy as jnp

def _softmax(x, axis=-1):
    return jax.nn.softmax(x, axis=axis)

def _gelu(x):
    return jax.nn.gelu(x, approximate=True)

def _silu(x):
    return jax.nn.silu(x)

def _sigmoid(x):
    return jax.nn.sigmoid(x)

def _layernorm(x, axis=-1, eps=1e-05):
    m = jnp.mean(x, axis=axis, keepdims=True)
    v = jnp.var(x, axis=axis, keepdims=True)
    return (x - m) / jnp.sqrt(v + eps)

def _scatter_add(tgt, idx, src, axis=0):
    return tgt.at[idx].add(src)

def _segment_sum(src, seg, n):
    return jax.ops.segment_sum(src, seg, n)
kernel_name = 'mk_macaron_d1_jaxref_r4_2ea647'

def setup_inputs(seed: int=0):
    np.random.seed(seed)
    _w = jnp.asarray

    def _L0_attn_setup():
        import jax, jax.numpy as jnp
        import numpy as np
        UNIQUE_OFFSETS = np.array([0, 1, 2, 3, 4, 6, 8, 12, 16, 24, 32, 48, 64, 96, 128, 192, 64, 96, 128, 192, 256, 384, 512, 768], dtype=np.int32)
        B, N, D, H = (1, 1024, 256, 16)
        HD = D // H
        key = jax.random.key(seed)
        ks = jax.random.split(key, 8)
        s = D ** (-0.5)
        return {'x': jax.random.normal(ks[0], (B, N, D), jnp.float32), 'Wqkv': jax.random.normal(ks[1], (D, 3 * D), jnp.float32) * s, 'bqkv': jnp.zeros((3 * D,), jnp.float32), 'Wout': jax.random.normal(ks[2], (D, D), jnp.float32) * s, 'bout': jnp.zeros((D,), jnp.float32), 'Wgate': jax.random.normal(ks[3], (D, D), jnp.float32) * s, 'bgate': jnp.full((D,), 2.0, jnp.float32), 'pos_bias': jax.random.normal(ks[4], (len(UNIQUE_OFFSETS), H), jnp.float32) * 0.1}
    _L0_attn_in = _L0_attn_setup()

    def _L0_ffn_setup():
        import jax, jax.numpy as jnp
        import numpy as np
        D_IN, D_HID = (256, 1024)

        def _ternary(key, shape):
            return jax.random.randint(key, shape, -1, 2).astype(jnp.float32)

        def _tlin(x, w, s):
            return jnp.einsum('bsi,oi->bso', x, w) * s
        key = jax.random.key(seed)
        ks = jax.random.split(key, 12)
        inv = lambda fan: 1.0 / np.sqrt(fan).astype(np.float32)
        return {'x': jax.random.normal(ks[0], (4, 512, D_IN), dtype=jnp.float32), 'w1_w': _ternary(ks[1], (D_HID, D_IN)), 'w1_s': jax.random.uniform(ks[2], (D_HID,), dtype=jnp.float32) * inv(D_IN), 'w2_w': _ternary(ks[3], (D_HID, D_IN)), 'w2_s': jax.random.uniform(ks[4], (D_HID,), dtype=jnp.float32) * inv(D_IN), 'h1_w': _ternary(ks[5], (D_HID, D_HID)), 'h1_s': jax.random.uniform(ks[6], (D_HID,), dtype=jnp.float32) * inv(D_HID), 'h2_w': _ternary(ks[7], (D_HID, D_HID)), 'h2_s': jax.random.uniform(ks[8], (D_HID,), dtype=jnp.float32) * inv(D_HID), 'w3_w': _ternary(ks[9], (D_IN, D_HID)), 'w3_s': jax.random.uniform(ks[10], (D_IN,), dtype=jnp.float32) * inv(D_HID)}
    _L0_ffn_in = _L0_ffn_setup()
    _d = {'L0_attn_x': _L0_attn_in['x'], 'L0_attn_Wqkv': _L0_attn_in['Wqkv'], 'L0_attn_bqkv': _L0_attn_in['bqkv'], 'L0_attn_Wout': _L0_attn_in['Wout'], 'L0_attn_bout': _L0_attn_in['bout'], 'L0_attn_Wgate': _L0_attn_in['Wgate'], 'L0_attn_bgate': _L0_attn_in['bgate'], 'L0_attn_pos_bias': _L0_attn_in['pos_bias'], 'L0_ffn_w1_w': _L0_ffn_in['w1_w'], 'L0_ffn_w1_s': _L0_ffn_in['w1_s'], 'L0_ffn_w2_w': _L0_ffn_in['w2_w'], 'L0_ffn_w2_s': _L0_ffn_in['w2_s'], 'L0_ffn_h1_w': _L0_ffn_in['h1_w'], 'L0_ffn_h1_s': _L0_ffn_in['h1_s'], 'L0_ffn_h2_w': _L0_ffn_in['h2_w'], 'L0_ffn_h2_s': _L0_ffn_in['h2_s'], 'L0_ffn_w3_w': _L0_ffn_in['w3_w'], 'L0_ffn_w3_s': _L0_ffn_in['w3_s']}
    _x0 = _d['L0_attn_x']
    _d['L0_attn_x'] = jax.random.normal(jax.random.fold_in(jax.random.key(seed), 1), (4, 1024, 256), dtype=_x0.dtype)
    del _x0
    return _d

def reference(L0_attn_x, L0_attn_Wqkv, L0_attn_bqkv, L0_attn_Wout, L0_attn_bout, L0_attn_Wgate, L0_attn_bgate, L0_attn_pos_bias, L0_ffn_w1_w, L0_ffn_w1_s, L0_ffn_w2_w, L0_ffn_w2_s, L0_ffn_h1_w, L0_ffn_h1_s, L0_ffn_h2_w, L0_ffn_h2_s, L0_ffn_w3_w, L0_ffn_w3_s):

    def _L0_attn_ref(x, Wqkv, bqkv, Wout, bout, Wgate, bgate, pos_bias):
        import jax, jax.numpy as jnp
        import numpy as np
        UNIQUE_OFFSETS = np.array([0, 1, 2, 3, 4, 6, 8, 12, 16, 24, 32, 48, 64, 96, 128, 192, 64, 96, 128, 192, 256, 384, 512, 768], dtype=np.int32)
        B, N, D, H = (1, 1024, 256, 16)
        HD = D // H
        b, n, d = x.shape
        scale = HD ** (-0.5)
        qkv = x @ Wqkv + bqkv
        q, k, v = jnp.split(qkv, 3, axis=-1)

        def heads(t):
            return t.reshape(b, n, H, HD).transpose(0, 2, 1, 3)
        q, k, v = (heads(q), heads(k), heads(v))
        deltas = jnp.asarray(UNIQUE_OFFSETS)
        idx = jnp.arange(n)[:, None] - deltas[None, :]
        valid = (idx >= 0).astype(x.dtype)[:, :, None]
        idxc = jnp.clip(idx, 0, n - 1)
        k_g = k[:, :, idxc, :] * valid
        v_g = v[:, :, idxc, :] * valid
        scores = jnp.einsum('bhnd,bhnod->bhno', q, k_g) * scale + pos_bias.T[None, :, None, :]
        attn = jax.nn.softmax(scores, axis=-1)
        out = jnp.einsum('bhno,bhnod->bhnd', attn, v_g)
        out_flat = out.transpose(0, 2, 1, 3).reshape(b, n, d)
        gate = jax.nn.sigmoid(x @ Wgate + bgate)
        return out_flat * gate @ Wout + bout

    def _L0_ffn_ref(x, w1_w, w1_s, w2_w, w2_s, h1_w, h1_s, h2_w, h2_s, w3_w, w3_s):
        import jax, jax.numpy as jnp
        import numpy as np
        D_IN, D_HID = (256, 1024)

        def _ternary(key, shape):
            return jax.random.randint(key, shape, -1, 2).astype(jnp.float32)

        def _tlin(x, w, s):
            return jnp.einsum('bsi,oi->bso', x, w) * s
        h = jax.nn.silu(_tlin(x, w1_w, w1_s)) * _tlin(x, w2_w, w2_s)
        h = jax.nn.gelu(_tlin(h, h1_w, h1_s), approximate=False)
        h = jax.nn.gelu(_tlin(h, h2_w, h2_s), approximate=False)
        return _tlin(h, w3_w, w3_s)
    x = L0_attn_x
    x = x + 0.5 * _L0_ffn_ref(_layernorm(x, axis=-1), L0_ffn_w1_w, L0_ffn_w1_s, L0_ffn_w2_w, L0_ffn_w2_s, L0_ffn_h1_w, L0_ffn_h1_s, L0_ffn_h2_w, L0_ffn_h2_s, L0_ffn_w3_w, L0_ffn_w3_s)
    x = x + _L0_attn_ref(_layernorm(x, axis=-1), L0_attn_Wqkv, L0_attn_bqkv, L0_attn_Wout, L0_attn_bout, L0_attn_Wgate, L0_attn_bgate, L0_attn_pos_bias)
    x = x + 0.5 * _L0_ffn_ref(_layernorm(x, axis=-1), L0_ffn_w1_w, L0_ffn_w1_s, L0_ffn_w2_w, L0_ffn_w2_s, L0_ffn_h1_w, L0_ffn_h1_s, L0_ffn_h2_w, L0_ffn_h2_s, L0_ffn_w3_w, L0_ffn_w3_s)
    return x

_drawn_inputs = setup_inputs


def setup_inputs(seed=0):
    import zlib

    import numpy as np

    out = dict(_drawn_inputs(seed))
    spreads = {'L0_attn_bqkv': (0.0, 0.1), 'L0_attn_bout': (0.0, 0.1), 'L0_attn_bgate': (2.0, 0.2)}
    factors = {}
    for name, (base, spread) in spreads.items():
        noise = np.random.default_rng([zlib.crc32(name.encode()), seed]).standard_normal(out[name].shape)
        drawn = base * np.exp(spread * noise) if base else spread * noise
        out[name] = jnp.asarray(drawn.astype(out[name].dtype))
    for name, factor in factors.items():
        out[name] = (out[name] * factor).astype(out[name].dtype)
    return out
```

```python
import concourse.bass as bass
from concourse import mybir
from contextlib import ExitStack

OFFSETS = [0, 1, 2, 3, 4, 6, 8, 12, 16, 24, 32, 48, 64, 96, 128, 192, 64, 96, 128, 192, 256, 384, 512, 768]
UNIQUE = sorted(set(OFFSETS))
TWICE = [o for o in UNIQUE if OFFSETS.count(o) == 2]
EPS = 1e-5


class Counts:

    def __init__(self, per_subtile):
        self.total = sum(per_subtile)
        self.before = [sum(per_subtile[:c]) for c in range(len(per_subtile))]

    def at(self, sub, k):
        return sub.batch * self.total + (self.before[sub.c] + k)


class Ffn:

    def __init__(self, half_number, parity, tile, second):
        self.h, self.p, self.tile, self.second = half_number, parity, tile, second

    def at(self, per_run, k):
        return self.h * (2 * per_run) + (self.p * per_run + k)


class Sub:

    def __init__(self, batch, c, per_batch):
        self.batch, self.c, self.per_batch = batch, c, per_batch

    def at(self, per_sub, k):
        return self.batch * (self.per_batch * per_sub) + (self.c * per_sub + k)


def macaron_kernel(nc, x, ffn_w, proj_w, out_w, cols, rows, masks, out):
    fp32, fp32r = mybir.dt.float32, mybir.dt.float32r
    ALU, ACT, AX = mybir.AluOpType, mybir.ActivationFunctionType, mybir.AxisListType

    P = 128
    B, N, D = x.shape
    HEADS = 16
    DH = D // HEADS
    KD = D // P
    HID = 1024
    KH = HID // P
    TT = 512
    NB = TT // P
    TILES = B * N // TT
    TPB = N // TT
    ST = 256
    SB = ST // P
    SUBS = N // ST
    NU, NE = len(UNIQUE), len(OFFSETS)
    ROWS = HEADS * NU
    GROUPS = [list(range(g, min(g + 8, NU))) for g in range(0, NU, 8)]
    FOLD_ROWS = P // HEADS
    SCALE = DH ** -0.5
    FIRST_TWICE = UNIQUE.index(TWICE[0]) * HEADS
    WBLK = 1024
    H_BLOCKS, IN_BLOCKS, OUT_BLOCKS = 2 * KH, 4, 2
    BLOCKS = H_BLOCKS + IN_BLOCKS + OUT_BLOCKS

    valid = [[j for j, o in enumerate(UNIQUE) if o < ST * (c + 1)] for c in range(SUBS)]
    groups_of = [[g for g in range(3) if GROUPS[g][0] in valid[c]] for c in range(SUBS)]
    per_offset = Counts([len(v) for v in valid])
    per_later_offset = Counts([len(v) - 1 for v in valid])
    per_pair = Counts([(len(v) + 1) // 2 for v in valid])
    per_half = Counts([1 if len(g) == 2 else 2 for g in groups_of])

    MM = 2 * KH + KH + KH + 2
    LO = 3 * KH

    x_rows = x.rearrange("b (t n p) d -> (b t) p n d", n=NB, p=P)
    x1 = nc.dram_tensor("x_after_ffn1", (TILES, P, NB, D), fp32)
    x2 = nc.dram_tensor("x_after_attention", (TILES, P, NB, D), fp32)
    out_rows = out.rearrange("b (t n p) d -> (b t) p n d", n=NB, p=P)
    hi_dram = nc.dram_tensor("weights_hi", (H_BLOCKS, P, WBLK), fp32)
    lo_dram = nc.dram_tensor("weights_lo", (BLOCKS, P, WBLK), fp32)

    ctx = ExitStack()
    with ctx:
        def sb(name, shape, dt=fp32):
            return ctx.enter_context(nc.sbuf_tensor(name, shape, dt))

        def sem(name):
            return ctx.enter_context(nc.semaphore(name))

        w_in = sb("w_in", [P, IN_BLOCKS, WBLK], fp32r)
        w_out3 = sb("w_out3", [P, OUT_BLOCKS, WBLK], fp32r)
        wring = sb("wring", [P, 4, WBLK], fp32r)
        wproj = sb("wproj", [P, KD, 4 * D])
        wo = sb("wo", [P, KD, D])
        colv = sb("colv", [P, 40])
        rowv = sb("rowv", [P, 2 * D + NE * HEADS])
        ident = sb("ident", [P, P])
        sel_in = sb("sel_in", [P, 15 * HEADS])
        sel_out = sb("sel_out", [P, 8, P], fp32r)
        half_neg = sb("half_neg", [P, NB])
        xf = sb("xf", [P, 2, NB, D])
        f_hat = sb("f_hat", [P, 2, D])
        fT_hi = sb("fT_hi", [P, KD, TT], fp32r)
        fT_lo = sb("fT_lo", [P, KD, TT], fp32r)
        h_hi = [sb(f"h_hi{i}", [P, KH, TT], fp32r) for i in range(2)]
        h_lo = [sb(f"h_lo{i}", [P, KH, TT], fp32r) for i in range(2)]
        f_gated = sb("f_gated", [P, 2, TT])
        f_tmp = sb("f_tmp", [P, 2, D])
        f_st = sb("f_st", [P, NB, 6])
        f_mo = sb("f_mo", [P, 5, NB])
        f_mean = sb("f_mean", [P, NB])
        f_var = sb("f_var", [P, NB])
        f_rs = sb("f_rs", [P, NB])
        xa = sb("xa", [P, 2, SB, D])
        a_hat = sb("a_hat", [P, SB, D])
        aT = sb("aT", [P, KD, ST])
        q = sb("q", [P, 2, ST])
        keys = sb("keys", [P, 2, N])
        vals = sb("vals", [P, 2, N])
        gate = sb("gate", [P, 2, ST])
        prod = sb("prod", [P, 4, 2, ST])
        fold = sb("fold", [P, 4, ST])
        sT = sb("sT", [P, 3, ST])
        S = sb("S", [P, SB, NE * HEADS])
        p_hi = sb("p_hi", [P, 3, ST], fp32r)
        p_lo = sb("p_lo", [P, 3, ST], fp32r)
        acc = sb("acc", [P, 2, ST])
        a_tmp = sb("a_tmp", [P, SB, D])
        a_st = sb("a_st", [P, SB, 6])
        a_mo = sb("a_mo", [P, 5, SB])
        a_mean = sb("a_mean", [P, SB])
        a_var = sb("a_var", [P, SB])
        a_rs = sb("a_rs", [P, SB])
        mx = sb("mx", [P, SB, HEADS])
        sm = sb("sm", [P, SB, HEADS])

        fb = [ctx.enter_context(nc.psum_tensor(f"f_bank{i}", [P, 512], fp32)) for i in range(4)]
        ab = [ctx.enter_context(nc.psum_tensor(f"a_bank{i}", [P, 512], fp32)) for i in range(4)]

        def w12(m, w, k):
            o = ((m % 2) * 4 + w * 2 + k) * P
            return w_in[:, m // 2, o:o + P]

        def scale_col(layer, m):
            return colv[:, layer * KH + m:layer * KH + m + 1]

        qkv_bias = [[colv[:, 32 + 2 * w + e:33 + 2 * w + e] for e in range(2)] for w in range(3)]
        gate_bias = [colv[:, 38 + e:39 + e] for e in range(2)]
        s3 = rowv[:, 0:D]
        bout = rowv[:, D:2 * D]
        pos = rowv[:, 2 * D:]

        s_const = sem("s_const")
        s_mask = sem("s_mask")
        s_stage = [sem(f"s_stage{i}") for i in range(2)]
        s_hi = sem("s_hi")
        s_lo = sem("s_lo")
        s_stored = [sem(f"s_stored{i}") for i in range(4)]
        s_sel = sem("s_sel")
        s_scaled = sem("s_scaled")
        s_neg = sem("s_neg")
        s_ring = [sem(f"s_ring{i}") for i in range(4)]
        f_loaded = [sem(f"f_loaded{i}") for i in range(2)]
        f_stored = [sem(f"f_stored{i}") for i in range(2)]
        f_stats, f_summed, f_squared = sem("f_stats"), sem("f_summed"), sem("f_squared")
        f_vareps, f_rstd = sem("f_vareps"), sem("f_rstd")
        f_norm, f_turned, f_thi, f_tlo = sem("f_norm"), sem("f_turned"), sem("f_thi"), sem("f_tlo")
        f_mm, f_silu, f_prod, f_phi = sem("f_mm"), sem("f_silu"), sem("f_prod"), sem("f_phi")
        f_gelu, f_lo, f_outs, f_x = sem("f_gelu"), sem("f_lo"), sem("f_outs"), sem("f_x")
        a_loaded = [sem(f"a_loaded{i}") for i in range(2)]
        a_stored = [sem(f"a_stored{i}") for i in range(2)]
        a_stats, a_summed, a_squared = sem("a_stats"), sem("a_summed"), sem("a_squared")
        a_vareps, a_rstd = sem("a_vareps"), sem("a_rstd")
        a_norm, a_turned, a_xT = sem("a_norm"), sem("a_turned"), sem("a_xT")
        a_proj, a_qkv, a_gexp = sem("a_proj"), sem("a_qkv"), sem("a_gexp")
        a_gone, a_gate = sem("a_gone"), sem("a_gate")
        a_qk, a_fold, a_scored = sem("a_qk"), sem("a_fold"), sem("a_scored")
        a_scopied, a_sturned, a_biased = sem("a_scopied"), sem("a_sturned"), sem("a_biased")
        a_max, a_less, a_exp, a_sum = sem("a_max"), sem("a_less"), sem("a_exp"), sem("a_sum")
        a_recip, a_probs, a_pturned = sem("a_recip"), sem("a_probs"), sem("a_pturned")
        a_phi, a_plo, a_spread_done = sem("a_phi"), sem("a_plo"), sem("a_spread_done")
        a_pv, a_acc, a_z = sem("a_pv"), sem("a_acc"), sem("a_z")
        a_wo, a_otmp, a_x = sem("a_wo"), sem("a_otmp"), sem("a_x")

        block = ctx.enter_context(nc.Block())

        def schedule(eng, do):
            def step(name, *args):
                if name in do:
                    do[name](*args)

            def ffn(r):
                step("f_load", r)
                step("f_norm", r)
                for m in range(KH + 1):
                    step("f_in", r, m)
                for layer in range(2):
                    for m in range(KH):
                        step("f_hidden", r, layer, m)
                for pair in range(2):
                    step("f_out", r, pair)

            def attention(a, tile, u):
                step("a_load", a, tile, u)
                step("a_norm", a)
                step("a_project", a)
                v = valid[a.c]
                for k in range(len(v) + 2):
                    if k < len(v):
                        step("a_score", a, k)
                    if k >= 2:
                        step("a_sum_heads", a, k - 2)
                step("a_softmax", a)
                step("a_spread", a, 0)
                for k in range(len(v)):
                    if k % 2 == 0 and k + 2 < len(v):
                        step("a_spread", a, k // 2 + 1)
                    step("a_weigh", a, k)
                step("a_out", a, tile, u)

            with eng.Fori(0, B) as b:
                for t in range(TPB):
                    tile = b * TPB + t
                    ffn(Ffn(tile, 0, tile, False))
                    for u in range(TT // ST):
                        attention(Sub(b, t * (TT // ST) + u, SUBS), tile, u)
                    ffn(Ffn(tile, 1, tile, True))

        ring_order = [("lo", H_BLOCKS + j, ("f_in", 2 * j)) for j in range(IN_BLOCKS)]
        for layer in range(2):
            for m in range(KH):
                ring_order += [("hi", layer * KH + m, ("f_hidden", layer, m)),
                               ("lo", layer * KH + m, ("f_hidden", layer, m))]
        ring_order += [("lo", H_BLOCKS + IN_BLOCKS + j, ("f_out", 0)) for j in range(OUT_BLOCKS)]
        RING = len(ring_order)
        SLOTS = 2
        assert RING % SLOTS == 0
        banks_after = [{"f_in": 4 * at[-1] // 2 + 4, "f_hidden": 2 * KH + at[-2] * KH + at[-1] + 1 if len(at) > 2 else 0,
                        "f_out": MM}[at[0]] for _, _, at in ring_order]
        of_step = {}
        for i, (_, _, at) in enumerate(ring_order):
            of_step.setdefault(at, []).append(i)

        def slot_filled(r, i):
            return r.at(16 * (RING // SLOTS), 16 * (i // SLOTS + 1))

        @block.sync
        def _(sp):
            sp.dma_start(colv[:, :], cols).then_inc(s_const, 16)
            sp.dma_start(rowv[:, :], rows.partition_broadcast(P)).then_inc(s_const, 16)
            sp.dma_start(ident[:, :], masks[:, 0:P]).then_inc(s_const, 16)
            sp.dma_start(sel_in[:, :], masks[:, P:P + 15 * HEADS]).then_inc(s_const, 16)
            sp.dma_start(wproj[:, :, :], proj_w).then_inc(s_const, 16)
            sp.dma_start(wo[:, :, :], out_w).then_inc(s_const, 16)
            sp.dma_start(prod[:, :, :, :].rearrange("p a e n -> p (a e n)")[:, 0:8 * P],
                         masks[:, P + 15 * HEADS:]).then_inc(s_mask, 16)

            def stage(i, slot):
                sp.dma_start(xf[:, slot, :, :].rearrange("p n d -> p (n d)"), ffn_w[i, :, :])\
                    .then_inc(s_stage[slot], 16)

            def keep_lo(i, s):
                sp.dma_start(lo_dram[i, :, :], h_lo[0][:, 2 * s:2 * s + 2, :].bitcast(fp32)).then_inc(s_stored[s], 16)

            stage(0, 0)
            stage(1, 1)
            with sp.Fori(0, H_BLOCKS // 4) as it:
                for s in range(4):
                    sp.wait_ge(s_lo, it * 4 + (s + 1))
                    sp.dma_start(hi_dram[it * 4 + s, :, :], h_hi[0][:, 2 * s:2 * s + 2, :].bitcast(fp32))\
                        .then_inc(s_stored[s], 16)
                    keep_lo(it * 4 + s, s)
                    stage(it * 4 + s + 2, s % 2)
            for i in range(H_BLOCKS, BLOCKS):
                sp.wait_ge(s_lo, i + 1)
                keep_lo(i, i % 4)
                if i + 2 < BLOCKS:
                    stage(i + 2, i % 2)
            for s in range(4):
                sp.wait_ge(s_stored[s], 32 * (H_BLOCKS // 4) + 16 * len(range(H_BLOCKS + s, BLOCKS, 4)))

            def ring(r, at):
                for i in of_step.get(at, []):
                    source, blk, _ = ring_order[i]
                    src = (hi_dram if source == "hi" else lo_dram)[blk, :, :]
                    sp.wait_ge(f_mm, r.at(MM, banks_after[i - SLOTS] if i >= SLOTS else 0))
                    sp.dma_start(wring[:, i % SLOTS, :].bitcast(fp32), src).then_inc(s_ring[i % SLOTS], 16)

            def f_load(r):
                sp.wait_ge(f_stored[r.p], r.h * 16)
                if r.second:
                    for u in range(2):
                        sp.wait_ge(a_stored[u], r.tile * 16 + 16)
                    sp.dma_start(xf[:, r.p, :, :], x2[r.tile, :, :, :]).then_inc(f_loaded[r.p], 16)
                else:
                    sp.dma_start(xf[:, r.p, :, :], x_rows[r.tile, :, :, :]).then_inc(f_loaded[r.p], 16)

            def f_out(r, pair):
                ring(r, ("f_out", pair))
                if pair == 1:
                    sp.wait_ge(f_x, r.at(2, 2))
                    dst = out_rows[r.tile, :, :, :] if r.second else x1[r.tile, :, :, :]
                    sp.dma_start(dst, xf[:, r.p, :, :]).then_inc(f_stored[r.p], 16)

            def a_load(a, tile, u):
                sp.wait_ge(f_stored[0], tile * 16 + 16)
                sp.wait_ge(a_stored[u], tile * 16)
                sp.dma_start(xa[:, u, :, :], x1[tile, :, u * SB:(u + 1) * SB, :]).then_inc(a_loaded[u], 16)

            def a_out(a, tile, u):
                sp.wait_ge(a_x, a.at(1, 1))
                sp.dma_start(x2[tile, :, u * SB:(u + 1) * SB, :], xa[:, u, :, :]).then_inc(a_stored[u], 16)

            schedule(sp, {
                "f_load": f_load, "f_out": f_out, "a_load": a_load, "a_out": a_out,
                "f_in": lambda r, m: ring(r, ("f_in", m)),
                "f_hidden": lambda r, layer, m: ring(r, ("f_hidden", layer, m)),
            })
            for p in range(2):
                sp.wait_ge(f_stored[p], 16 * TILES)

        @block.gpsimd
        def _(pool):
            pool.memset(half_neg[:, :], -0.5).then_inc(s_neg, 1)
            pool.wait_ge(s_neg, 1)

            def f_norm_(r):
                pool.wait_ge(f_vareps, r.at(1, 1))
                pool.tensor_tensor(f_rs[:, :], f_var[:, :], half_neg[:, :], ALU.pow).then_inc(f_rstd, 1)

            def a_norm_(a):
                pool.wait_ge(a_vareps, a.at(1, 1))
                pool.tensor_tensor(a_rs[:, :], a_var[:, :], half_neg[:, 0:SB], ALU.pow).then_inc(a_rstd, 1)

            def a_score(a, k):
                lo = max(0, UNIQUE[valid[a.c][k]] - ST * a.c)
                pool.wait_ge(a_qk, per_offset.at(a, k + 1))
                if k >= 4:
                    pool.wait_ge(a_scored, per_offset.at(a, k - 3))
                else:
                    pool.wait_ge(a_scored, per_offset.at(a, 0))
                last = pool.tensor_tensor(fold[:, k % 4, lo:ST], prod[:, k % 4, 0, lo:ST],
                                          prod[:, k % 4, 1, lo:ST], ALU.add)
                if lo and valid[a.c][k] % 8 == 0:
                    last = pool.memset(fold[:, k % 4, 0:lo], 0.0)
                last.then_inc(a_fold, 1)

            def a_weigh(a, k):
                if k == 0:
                    return
                lo = max(0, UNIQUE[valid[a.c][k]] - ST * a.c)
                pool.wait_ge(a_pv, per_later_offset.at(a, k))
                pool.wait_ge(a_acc, per_offset.at(a, k))
                pool.tensor_tensor(acc[:, :, lo:ST], acc[:, :, lo:ST], prod[:, k % 4, :, lo:ST], ALU.add)\
                    .then_inc(a_acc, 1)

            schedule(pool, {"f_norm": f_norm_, "a_norm": a_norm_, "a_score": a_score, "a_weigh": a_weigh})

        @block.scalar
        def _(act):
            act.wait_ge(s_mask, 16)
            act.activation(sel_out[:, :, :].rearrange("p j f -> p (j f)"),
                           prod[:, :, :, :].rearrange("p a e n -> p (a e n)")[:, 0:8 * P], ACT.Copy)\
                .then_inc(s_sel, 1)

            def cut_hi(i, s, stage_value, dst):
                act.wait_ge(s_stage[s % 2], stage_value)
                act.activation(dst, xf[:, s % 2, :, :].rearrange("p n d -> p (n d)"), ACT.Copy).then_inc(s_hi, 1)

            with act.Fori(0, H_BLOCKS // 4) as it:
                for s in range(4):
                    act.wait_ge(s_stored[s], it * 32)
                    cut_hi(it * 4 + s, s, it * 32 + 16 * (s // 2 + 1),
                           h_hi[0][:, 2 * s:2 * s + 2, :].rearrange("p a n -> p (a n)"))
            for i in range(H_BLOCKS, BLOCKS):
                j = i - H_BLOCKS
                dst = w_in[:, j, :] if j < IN_BLOCKS else w_out3[:, j - IN_BLOCKS, :]
                cut_hi(i, i % 4, 16 * (i // 2 + 1), dst)
            act.wait_ge(s_scaled, 3)

            def f_norm_(r):
                for bp in range(2):
                    act.wait_ge(f_turned, r.at(2, bp + 1))
                    act.activation(fT_hi[:, :, bp * ST:(bp + 1) * ST],
                                   fb[bp][:, :].rearrange("p (k n) -> p k n", k=KD), ACT.Copy).then_inc(f_thi, 1)

            def f_in(r, m):
                if m < KH:
                    bank = fb[(2 * m) % 4]
                    act.wait_ge(f_mm, r.at(MM, 2 * m + 1))
                    act.activation(f_gated[:, m % 2, :], bank[:, :], ACT.Silu, scale=scale_col(0, m)).then_inc(f_silu, 1)
                if m > 0:
                    act.wait_ge(f_prod, r.at(KH, m))
                    act.activation(h_hi[r.p][:, m - 1, :], fb[(2 * m - 1) % 4][:, :], ACT.Copy).then_inc(f_phi, 1)

            def f_hidden(r, layer, m):
                n = 2 * KH + layer * KH + m
                bank, dst = fb[n % 4], h_hi[(r.p + 1 + layer) % 2]
                act.wait_ge(f_mm, r.at(MM, n + 1))
                act.activation(dst[:, m, :], bank[:, :], ACT.Gelu, scale=scale_col(2 + layer, m))
                act.activation(bank[:, :], bank[:, :], ACT.Gelu, scale=scale_col(2 + layer, m)).then_inc(f_gelu, 1)

            def a_norm_(a):
                act.wait_ge(a_turned, a.at(1, 1))
                act.activation(aT[:, :, :].rearrange("p k n -> p (k n)"), ab[0][:, :], ACT.Copy).then_inc(a_xT, 1)

            def a_project(a):
                s0 = ST * a.c
                for w, dst in enumerate((q[:, :, :], keys[:, :, s0:s0 + ST], vals[:, :, s0:s0 + ST])):
                    act.wait_ge(a_proj, a.at(4, w + 1))
                    for e in range(2):
                        last = act.activation(dst[:, e, :], ab[1 + w][:, e * ST:(e + 1) * ST], ACT.Identity,
                                              bias=qkv_bias[w][e], scale=SCALE if w == 0 else 1.0)
                    last.then_inc(a_qkv, 1)
                act.wait_ge(a_proj, a.at(4, 4))
                for e in range(2):
                    last = act.activation(gate[:, e, :], ab[0][:, e * ST:(e + 1) * ST], ACT.Exp,
                                          bias=gate_bias[e], scale=-1.0)
                last.then_inc(a_gexp, 1)

            def a_softmax(a):
                v, gs = valid[a.c], groups_of[a.c]
                act.wait_ge(a_scored, per_offset.at(a, 16))
                act.activation(sT[:, 0:2, :].rearrange("p g n -> p (g n)"), ab[1][:, :], ACT.Copy).then_inc(a_scopied, 1)
                if len(gs) > 2:
                    act.wait_ge(a_scored, per_offset.at(a, len(v)))
                    act.activation(sT[0:64, 2, :], ab[2][0:64, 0:ST], ACT.Copy).then_inc(a_scopied, 1)
                act.wait_ge(a_less, a.at(1, 1))
                act.activation(S[:, :, :], S[:, :, :], ACT.Exp).then_inc(a_exp, 1)
                act.wait_ge(a_pturned, per_half.at(a, 1))
                act.activation(p_hi[:, 0:2, :].rearrange("p g n -> p (g n)"), ab[1][:, :], ACT.Copy).then_inc(a_phi, 1)
                if len(gs) > 2:
                    act.wait_ge(a_pturned, per_half.at(a, 2))
                    act.activation(p_hi[0:64, 2, :], ab[2][0:64, 0:ST], ACT.Copy).then_inc(a_phi, 1)

            schedule(act, {"f_norm": f_norm_, "f_in": f_in, "f_hidden": f_hidden,
                           "a_norm": a_norm_, "a_project": a_project, "a_softmax": a_softmax})

        @block.vector
        def _(dve):
            dve.wait_ge(s_const, 16 * 6)
            dve.tensor_scalar(s3, s3, 0.5, None, ALU.mult).then_inc(s_scaled, 1)
            dve.tensor_scalar(colv[:, 32:34], colv[:, 32:34], SCALE, None, ALU.mult).then_inc(s_scaled, 1)
            dve.tensor_scalar(colv[:, 38:40], colv[:, 38:40], -1.0, None, ALU.mult).then_inc(s_scaled, 1)

            def cut_lo(s, hi_value, hi):
                dve.wait_ge(s_hi, hi_value)
                dve.tensor_tensor(h_lo[0][:, 2 * s:2 * s + 2, :].rearrange("p a n -> p (a n)"),
                                  xf[:, s % 2, :, :].rearrange("p n d -> p (n d)"), hi.bitcast(fp32),
                                  ALU.subtract).then_inc(s_lo, 1)

            with dve.Fori(0, H_BLOCKS // 4) as it:
                for s in range(4):
                    dve.wait_ge(s_stored[s], it * 32)
                    cut_lo(s, it * 4 + (s + 1), h_hi[0][:, 2 * s:2 * s + 2, :].rearrange("p a n -> p (a n)"))
            for i in range(H_BLOCKS, BLOCKS):
                j = i - H_BLOCKS
                hi = w_in[:, j, :] if j < IN_BLOCKS else w_out3[:, j - IN_BLOCKS, :]
                dve.wait_ge(s_stored[i % 4], 32 * (H_BLOCKS // 4) + 16 * (j // 4))
                cut_lo(i % 4, i + 1, hi)
            dve.wait_ge(s_scaled, 3)

            def moments(run, st, mo, mean, var, stats, summed, squared, vareps):
                even, odd = (1, 2), (4, 5)
                dve.wait_ge(stats, run.at(1, 1))
                dve.tensor_tensor(mo[:, 0, :], st[:, :, even[0]], st[:, :, odd[0]], ALU.add)
                dve.tensor_tensor(mo[:, 1, :], st[:, :, even[0]], st[:, :, odd[0]], ALU.subtract)
                dve.tensor_tensor(mo[:, 2, :], st[:, :, even[1]], st[:, :, odd[1]], ALU.add).then_inc(summed, 1)
                dve.wait_ge(summed, run.at(1, 1))
                dve.tensor_scalar(mean[:, :], mo[:, 0, :], 0.5, None, ALU.mult)
                dve.tensor_tensor(mo[:, 3, :], mo[:, 1, :], mo[:, 1, :], ALU.mult)
                dve.tensor_scalar(mo[:, 4, :], mo[:, 2, :], 1.0 / D, EPS, ALU.mult, ALU.add).then_inc(squared, 1)
                dve.wait_ge(squared, run.at(1, 1))
                dve.scalar_tensor_tensor(var[:, :], mo[:, 3, :], 0.25, mo[:, 4, :], ALU.mult, ALU.add)\
                    .then_inc(vareps, 1)

            def f_norm_(r):
                dve.wait_ge(f_loaded[r.p], r.h * 16 + 16 + 0)
                for n in range(NB):
                    last = dve.bn_stats(f_st[:, n, :], xf[:, r.p, n, :])
                last.then_inc(f_stats, 1)
                moments(r, f_st, f_mo, f_mean, f_var, f_stats, f_summed, f_squared, f_vareps)
                dve.wait_ge(f_rstd, r.at(1, 1))
                for bp in range(2):
                    if bp:
                        dve.wait_ge(f_turned, r.at(2, 1))
                    for n in range(2):
                        i = 2 * bp + n
                        last = dve.tensor_scalar(f_hat[:, n, :], xf[:, r.p, i, :], f_mean[:, i:i + 1],
                                                 f_rs[:, i:i + 1], ALU.subtract, ALU.mult)
                    last.then_inc(f_norm, 1)
                for bp in range(2):
                    dve.wait_ge(f_thi, r.at(2, bp + 1))
                    cols_ = slice(bp * ST, (bp + 1) * ST)
                    dve.tensor_tensor(fT_lo[:, :, cols_], fb[bp][:, :].rearrange("p (k n) -> p k n", k=KD),
                                      fT_hi[:, :, cols_].bitcast(fp32), ALU.subtract).then_inc(f_tlo, 1)

            def f_in(r, m):
                if m < KH:
                    g, u = f_gated[:, m % 2, :], fb[(2 * m + 1) % 4]
                    dve.wait_ge(f_silu, r.at(KH, m + 1))
                    dve.wait_ge(f_mm, r.at(MM, 2 * m + 2))
                    dve.scalar_tensor_tensor(u[:, :], u[:, :], scale_col(1, m), g, ALU.mult, ALU.mult)\
                        .then_inc(f_prod, 1)
                if m > 0:
                    dve.wait_ge(f_phi, r.at(KH, m))
                    dve.tensor_tensor(h_lo[r.p][:, m - 1, :], fb[(2 * m - 1) % 4][:, :],
                                      h_hi[r.p][:, m - 1, :].bitcast(fp32), ALU.subtract).then_inc(f_lo, 1)

            def f_hidden(r, layer, m):
                n = 2 * KH + layer * KH + m
                i = (r.p + 1 + layer) % 2
                dve.wait_ge(f_gelu, r.at(2 * KH, layer * KH + m + 1))
                dve.tensor_tensor(h_lo[i][:, m, :], fb[n % 4][:, :], h_hi[i][:, m, :].bitcast(fp32),
                                  ALU.subtract).then_inc(f_lo, 1)

            def f_out(r, pair):
                n = 4 * KH + pair
                dve.wait_ge(f_mm, r.at(MM, n + 1))
                dve.wait_ge(f_x, r.at(2, pair))
                dve.tensor_tensor(f_tmp[:, :, :], fb[n % 4][:, :].rearrange("p (n d) -> p n d", n=2),
                                  s3.unsqueeze(1).to_broadcast([P, 2, D]), ALU.mult).then_inc(f_outs, 1)
                dve.wait_ge(f_outs, r.at(2, pair + 1))
                rows_ = xf[:, r.p, 2 * pair:2 * pair + 2, :]
                dve.tensor_tensor(rows_, rows_, f_tmp[:, :, :], ALU.add).then_inc(f_x, 1)

            def a_norm_(a):
                u = a.c % 2
                dve.wait_ge(a_loaded[u], a.batch * (16 * TPB) + 16 * (a.c // 2 + 1))
                for n in range(SB):
                    last = dve.bn_stats(a_st[:, n, :], xa[:, u, n, :])
                last.then_inc(a_stats, 1)
                moments(a, a_st, a_mo, a_mean, a_var, a_stats, a_summed, a_squared, a_vareps)
                dve.wait_ge(a_rstd, a.at(1, 1))
                for n in range(SB):
                    last = dve.tensor_scalar(a_hat[:, n, :], xa[:, u, n, :], a_mean[:, n:n + 1],
                                             a_rs[:, n:n + 1], ALU.subtract, ALU.mult)
                last.then_inc(a_norm, 1)

            def a_project(a):
                dve.wait_ge(a_gexp, a.at(1, 1))
                dve.tensor_scalar(gate[:, :, :], gate[:, :, :], 1.0, None, ALU.add).then_inc(a_gone, 1)
                dve.wait_ge(a_gone, a.at(1, 1))
                dve.reciprocal(gate[:, :, :], gate[:, :, :]).then_inc(a_gate, 1)

            def shifted(a, k):
                s0, o = ST * a.c, UNIQUE[valid[a.c][k]]
                lo = max(0, o - s0)
                return lo, slice(s0 - o + lo, s0 - o + ST)

            def a_score(a, k):
                lo, back = shifted(a, k)
                if k == 0:
                    dve.wait_ge(a_qkv, a.at(3, 3))
                if k >= 4:
                    dve.wait_ge(a_fold, per_offset.at(a, k - 3))
                dve.tensor_tensor(prod[:, k % 4, :, lo:ST], q[:, :, lo:ST], keys[:, :, back], ALU.mult)\
                    .then_inc(a_qk, 1)

            def a_softmax(a):
                gs = groups_of[a.c]
                for n in range(SB):
                    bank = ab[3] if n == 0 else ab[0]
                    dve.wait_ge(a_sturned, a.at(SB, n + 1))
                    w = ROWS if len(gs) > 2 else 2 * P
                    dve.tensor_tensor(S[:, n, 0:w], bank[:, 0:w], pos[:, 0:w], ALU.add)
                    if w < ROWS:
                        dve.tensor_copy(S[:, n, w:ROWS], pos[:, w:ROWS])
                    dve.tensor_tensor(S[:, n, ROWS:], bank[:, FIRST_TWICE:FIRST_TWICE + len(TWICE) * HEADS],
                                      pos[:, ROWS:], ALU.add).then_inc(a_biased, 1)
                by_head = S[:, :, :].rearrange("p n (e h) -> p n h e", h=HEADS)
                by_entry = S[:, :, :].rearrange("p n (e h) -> p n e h", h=HEADS)
                dve.wait_ge(a_biased, a.at(SB, SB))
                dve.tensor_reduce(mx[:, :, :], by_head, AX.X, ALU.max).then_inc(a_max, 1)
                dve.wait_ge(a_max, a.at(1, 1))
                dve.tensor_tensor(by_entry, by_entry, mx[:, :, :].unsqueeze(2).to_broadcast([P, SB, NE, HEADS]),
                                  ALU.subtract).then_inc(a_less, 1)
                dve.wait_ge(a_exp, a.at(1, 1))
                dve.tensor_reduce(sm[:, :, :], by_head, AX.X, ALU.add).then_inc(a_sum, 1)
                dve.wait_ge(a_sum, a.at(1, 1))
                both = S[:, :, FIRST_TWICE:FIRST_TWICE + len(TWICE) * HEADS]
                dve.tensor_tensor(both, both, S[:, :, ROWS:], ALU.add)
                dve.reciprocal(sm[:, :, :], sm[:, :, :]).then_inc(a_recip, 1)
                dve.wait_ge(a_recip, a.at(1, 1))
                probs = S[:, :, 0:ROWS].rearrange("p n (e h) -> p n e h", h=HEADS)
                dve.tensor_tensor(probs, probs, sm[:, :, :].unsqueeze(2).to_broadcast([P, SB, NU, HEADS]),
                                  ALU.mult).then_inc(a_probs, 1)
                dve.wait_ge(a_phi, per_half.at(a, 1))
                dve.tensor_tensor(p_lo[:, 0:2, :].rearrange("p g n -> p (g n)"), ab[1][:, :],
                                  p_hi[:, 0:2, :].rearrange("p g n -> p (g n)").bitcast(fp32), ALU.subtract)\
                    .then_inc(a_plo, 1)
                if len(gs) > 2:
                    dve.wait_ge(a_phi, per_half.at(a, 2))
                    dve.tensor_tensor(p_lo[0:64, 2, :], ab[2][0:64, 0:ST], p_hi[0:64, 2, :].bitcast(fp32),
                                      ALU.subtract).then_inc(a_plo, 1)

            def a_weigh(a, k):
                lo, back = shifted(a, k)
                bank = ab[(3, 0, 1)[k // 2 % 3]]
                if k % 2 == 0:
                    dve.wait_ge(a_spread_done, per_pair.at(a, k // 2 + 1))
                if k >= 5:
                    dve.wait_ge(a_acc, per_offset.at(a, k - 3))
                spread = bank[:, (k % 2) * ST + lo:(k % 2 + 1) * ST].unsqueeze(1).to_broadcast([P, 2, ST - lo])
                dst = acc[:, :, :] if k == 0 else prod[:, k % 4, :, lo:ST]
                dve.tensor_tensor(dst, vals[:, :, back], spread, ALU.mult).then_inc(a_acc if k == 0 else a_pv, 1)

            def a_out(a, tile, u):
                dve.wait_ge(a_acc, per_offset.at(a, len(valid[a.c])))
                if True:
                    dve.wait_ge(a_gate, a.at(1, 1))
                dve.tensor_tensor(acc[:, :, :], acc[:, :, :], gate[:, :, :], ALU.mult).then_inc(a_z, 1)
                rows_ = xa[:, u, :, :]
                dve.wait_ge(a_wo, a.at(1, 1))
                dve.tensor_tensor(a_tmp[:, :, :], ab[2][:, :].rearrange("p (n d) -> p n d", n=SB), rows_,
                                  ALU.add).then_inc(a_otmp, 1)
                dve.wait_ge(a_otmp, a.at(1, 1))
                dve.tensor_tensor(rows_, a_tmp[:, :, :], bout.unsqueeze(1).to_broadcast([P, SB, D]), ALU.add)\
                    .then_inc(a_x, 1)

            schedule(dve, {"f_norm": f_norm_, "f_in": f_in, "f_hidden": f_hidden, "f_out": f_out,
                           "a_norm": a_norm_, "a_project": a_project, "a_score": a_score,
                           "a_softmax": a_softmax, "a_weigh": a_weigh, "a_out": a_out})

        @block.tensor
        def _(pe):
            pe.wait_ge(s_const, 16 * 6)
            pe.wait_ge(s_sel, 1)
            pe.wait_ge(s_lo, BLOCKS)

            def lo_block(r, i):
                pe.wait_ge(s_ring[i % SLOTS], slot_filled(r, i))
                return wring[:, i % SLOTS, :]

            def f_norm_(r):
                for bp in range(2):
                    pe.wait_ge(f_norm, r.at(2, bp + 1))
                    for kc in range(KD):
                        for n in range(2):
                            last = pe.transpose(fb[bp][:, kc * ST + n * P:kc * ST + (n + 1) * P],
                                                f_hat[:, n, kc * P:(kc + 1) * P], ident[:, :])
                    last.then_inc(f_turned, 1)

            def f_in(r, m):
                if m == KH:
                    return
                lo = None
                if m % 2 == 0:
                    lo_block(r, of_step[("f_in", m)][0])
                lo = wring[:, of_step[("f_in", m - m % 2)][0] % SLOTS, :]
                if m == 0:
                    pe.wait_ge(f_tlo, r.at(2, 2))
                for w in range(2):
                    n = 2 * m + w
                    bank = fb[n % 4]
                    if n == 2:
                        pe.wait_ge(f_outs, r.at(2, 0))
                    elif n >= 4:
                        pe.wait_ge(f_lo if w else f_silu, r.at(LO if w else KH, m - 1))
                    for k in range(KD):
                        pe.matmul(bank[:, :], w12(m, w, k), fT_hi[:, k, :], start=(k == 0), stop=False)
                        pe.matmul(bank[:, :], w12(m, w, k), fT_lo[:, k, :], start=False, stop=False)
                    for k in range(KD):
                        o = ((m % 2) * 4 + w * 2 + k) * P
                        last = pe.matmul(bank[:, :], lo[:, o:o + P], fT_hi[:, k, :], start=False, stop=(k == KD - 1))
                    last.then_inc(f_mm, 1)

            def f_hidden(r, layer, m):
                n = 2 * KH + layer * KH + m
                src = (r.p + layer) % 2
                bank = fb[n % 4]
                i_hi, i_lo = of_step[("f_hidden", layer, m)]
                hi = lo_block(r, i_hi)
                if n - 4 >= 2 * KH:
                    pe.wait_ge(f_lo, r.at(LO, n - 4 - KH + 1))
                elif (n - 4) % 2:
                    pe.wait_ge(f_lo, r.at(LO, (n - 4) // 2 + 1))
                else:
                    pe.wait_ge(f_silu, r.at(KH, (n - 4) // 2 + 1))
                for k in range(KH):
                    if m == 0:
                        pe.wait_ge(f_lo, r.at(LO, layer * KH + k + 1))
                    w = hi[:, k * P:(k + 1) * P]
                    pe.matmul(bank[:, :], w, h_hi[src][:, k, :], start=(k == 0), stop=False)
                    pe.matmul(bank[:, :], w, h_lo[src][:, k, :], start=False, stop=False)
                lo = lo_block(r, i_lo)
                for k in range(KH):
                    last = pe.matmul(bank[:, :], lo[:, k * P:(k + 1) * P], h_hi[src][:, k, :],
                                     start=False, stop=(k == KH - 1))
                last.then_inc(f_mm, 1)

            def f_out(r, pair):
                n = 4 * KH + pair
                bank = fb[n % 4]
                i0, i1 = of_step[("f_out", 0)]
                if pair == 0:
                    lo_block(r, i0)
                    lo_block(r, i1)
                    pe.wait_ge(f_lo, r.at(LO, LO))
                for half in range(2):
                    t = slice((2 * pair + half) * P, (2 * pair + half + 1) * P)
                    to = bank[:, half * D:(half + 1) * D]
                    for k in range(KH):
                        w = w_out3[:, k // 4, (k % 4) * D:(k % 4 + 1) * D]
                        w_lo = wring[:, (i0, i1)[k // 4] % SLOTS, (k % 4) * D:(k % 4 + 1) * D]
                        pe.matmul(to, h_hi[r.p][:, k, t], w, start=(k == 0), stop=False)
                        pe.matmul(to, h_lo[r.p][:, k, t], w, start=False, stop=False)
                        last = pe.matmul(to, h_hi[r.p][:, k, t], w_lo, start=False, stop=(k == KH - 1))
                last.then_inc(f_mm, 1)

            def a_norm_(a):
                pe.wait_ge(a_norm, a.at(1, 1))
                for kc in range(KD):
                    for n in range(SB):
                        last = pe.transpose(ab[0][:, kc * ST + n * P:kc * ST + (n + 1) * P],
                                            a_hat[:, n, kc * P:(kc + 1) * P], ident[:, :])
                last.then_inc(a_turned, 1)

            def a_project(a):
                pe.wait_ge(a_xT, a.at(1, 1))
                for w in range(4):
                    if w == 1:
                        pe.wait_ge(a_otmp, a.at(1, 0))
                    bank = ab[(1, 2, 3, 0)[w]]
                    for e in range(2):
                        for k in range(KD):
                            last = pe.matmul(bank[:, e * ST:(e + 1) * ST],
                                             wproj[:, k, w * D + e * P:w * D + (e + 1) * P], aT[:, k, :],
                                             start=(k == 0), stop=(k == KD - 1))
                    last.then_inc(a_proj, 1)

            def a_sum_heads(a, k):
                j = valid[a.c][k]
                g, jl = j // 8, j % 8
                v = valid[a.c]
                final = k + 1 == len(v) or v[k + 1] // 8 != g
                lo = 0 if jl == 0 else max(0, UNIQUE[j] - ST * a.c)
                rows_ = P if g < 2 else len(GROUPS[g]) * HEADS
                bank = ab[1 + g // 2]
                o = (7 - jl) * HEADS
                pe.wait_ge(a_fold, per_offset.at(a, k + 1))
                pe.matmul(bank[0:rows_, (g % 2) * ST + lo:(g % 2 + 1) * ST], sel_in[:, o:o + rows_],
                          fold[:, k % 4, lo:ST], start=(jl == 0), stop=final).then_inc(a_scored, 1)

            def a_softmax(a):
                gs = groups_of[a.c]
                pe.wait_ge(a_scopied, per_half.at(a, 2 if len(gs) > 2 else 1))
                for n in range(SB):
                    bank = ab[3] if n == 0 else ab[0]
                    for g in gs:
                        rows_ = P if g < 2 else 64
                        last = pe.transpose(bank[:, g * P:g * P + rows_], sT[0:rows_, g, n * P:(n + 1) * P],
                                            ident[0:rows_, 0:rows_])
                    last.then_inc(a_sturned, 1)
                pe.wait_ge(a_probs, a.at(1, 1))
                for n in range(SB):
                    for g in range(2):
                        last = pe.transpose(ab[1][:, g * ST + n * P:g * ST + (n + 1) * P],
                                            S[:, n, g * P:(g + 1) * P], ident[:, :])
                last.then_inc(a_pturned, 1)
                if len(gs) > 2:
                    for n in range(SB):
                        last = pe.transpose(ab[2][0:64, n * P:(n + 1) * P], S[:, n, 2 * P:2 * P + 64], ident[:, :])
                    last.then_inc(a_pturned, 1)

            def a_spread(a, pair):
                v = valid[a.c]
                bank = ab[(3, 0, 1)[pair % 3]]
                if pair == 0:
                    pe.wait_ge(a_plo, per_half.at(a, 2 if len(groups_of[a.c]) > 2 else 1))
                if pair >= 3:
                    pe.wait_ge(a_pv, per_later_offset.at(a, 2 * (pair - 3) + 1))
                for k in range(2 * pair, min(2 * pair + 2, len(v))):
                    g, jl = v[k] // 8, v[k] % 8
                    rows_ = P if g < 2 else 64
                    to = bank[:, (k % 2) * ST:(k % 2 + 1) * ST]
                    pe.matmul(to, sel_out[0:rows_, jl, :], p_hi[0:rows_, g, :], start=True, stop=False)
                    last = pe.matmul(to, sel_out[0:rows_, jl, :], p_lo[0:rows_, g, :], start=False, stop=True)
                last.then_inc(a_spread_done, 1)

            

            def a_out(a, tile, u):
                pe.wait_ge(a_z, a.at(1, 1))
                for n in range(SB):
                    for e in range(2):
                        last = pe.matmul(ab[2][:, n * D:(n + 1) * D], acc[:, e, n * P:(n + 1) * P], wo[:, e, :],
                                         start=(e == 0), stop=(e == 1))
                last.then_inc(a_wo, 1)

            schedule(pe, {"f_norm": f_norm_, "f_in": f_in, "f_hidden": f_hidden, "f_out": f_out,
                          "a_norm": a_norm_, "a_project": a_project, "a_sum_heads": a_sum_heads,
                          "a_softmax": a_softmax, "a_spread": a_spread, "a_out": a_out})


def _lay_out(inputs):
    import numpy as np
    g = {k: np.asarray(v) for k, v in inputs.items()}
    P, heads, dh, d, hid = 128, 16, 16, 256, 1024
    kh, kd = hid // P, d // P
    blocks = []
    for n in ("h1", "h2"):
        w = g[f"L0_ffn_{n}_w"].reshape(kh, P, kh, P)
        blocks.append(w.transpose(0, 3, 2, 1).reshape(kh, P, kh * P))
    w12 = np.stack([g["L0_ffn_w1_w"], g["L0_ffn_w2_w"]]).reshape(2, kh // 2, 2, P, kd, P)
    blocks.append(w12.transpose(1, 5, 2, 0, 4, 3).reshape(kh // 2, P, 8 * P))
    w3 = g["L0_ffn_w3_w"].reshape(d, 2, 4, P)
    blocks.append(w3.transpose(1, 3, 2, 0).reshape(2, P, 4 * d))
    ffn_w = np.concatenate(blocks)

    def split_heads(a, axis):
        s = a.shape
        a = a.reshape(s[:axis] + (-1, heads, 2, dh // 2) + s[axis + 1:])
        return np.moveaxis(a, axis + 2, axis + 1).reshape(s)

    proj = np.concatenate([split_heads(g["L0_attn_Wqkv"], 1), split_heads(g["L0_attn_Wgate"], 1)], axis=1)
    proj_w = proj.reshape(kd, P, 4 * d).transpose(1, 0, 2)
    out_w = split_heads(g["L0_attn_Wout"], 0).reshape(2, P, d).transpose(1, 0, 2)
    scales = [g[f"L0_ffn_{n}_s"].reshape(kh, P) for n in ("w1", "w2", "h1", "h2")]
    cols = np.concatenate(scales + [split_heads(g["L0_attn_bqkv"], 0).reshape(6, P),
                                    split_heads(g["L0_attn_bgate"], 0).reshape(2, P)]).T
    first = [OFFSETS.index(o) for o in UNIQUE]
    second = [len(OFFSETS) - 1 - OFFSETS[::-1].index(o) for o in TWICE]
    rows = np.concatenate([g["L0_ffn_w3_s"], g["L0_attn_bout"], g["L0_attn_pos_bias"][first + second].reshape(-1)])
    masks = np.zeros((P, P + 15 * heads + 8 * P), np.float32)
    p = np.arange(P)
    masks[p, p] = 1.0
    masks[p, P + 7 * heads + p // 8] = 1.0
    for j in range(8):
        f = np.arange(P)
        masks[heads * j + f // 8, P + 15 * heads + j * P + f] = 1.0
    return {"x": g["L0_attn_x"], "ffn_w": ffn_w, "proj_w": proj_w, "out_w": out_w, "cols": cols,
            "rows": rows, "masks": masks}


def kernel(**inputs):
    import numpy as np
    import concourse.bacc as bacc
    from concourse.bass_utils import run_bass_kernel_spmd

    nc = bacc.Bacc("TRN2", target_bir_lowering=False, num_devices=1)
    arrays, args = {}, []
    for name, a in _lay_out(inputs).items():
        a = np.ascontiguousarray(a)
        arrays[f"in_{name}"] = a
        args.append(nc.dram_tensor(f"in_{name}", a.shape, mybir.dt.from_np(a.dtype), kind="ExternalInput").ap())
    shape = arrays["in_x"].shape
    args.append(nc.dram_tensor("out_x", shape, mybir.dt.float32, kind="ExternalOutput").ap())
    macaron_kernel(nc, *args)
    r = run_bass_kernel_spmd(nc, [arrays], core_ids=[0])
    return r.results[0]["out_x"]
```

```python
import concourse.bass as bass
from concourse import mybir
from contextlib import ExitStack

OFFSETS = [0, 1, 2, 3, 4, 6, 8, 12, 16, 24, 32, 48, 64, 96, 128, 192, 64, 96, 128, 192, 256, 384, 512, 768]
UNIQUE = sorted(set(OFFSETS))
TWICE = [o for o in UNIQUE if OFFSETS.count(o) == 2]
EPS = 1e-5


class Counts:

    def __init__(self, per_subtile):
        self.total = sum(per_subtile)
        self.before = [sum(per_subtile[:c]) for c in range(len(per_subtile))]

    def at(self, sub, k):
        return sub.batch * self.total + (self.before[sub.c] + k)


class Ffn:

    def __init__(self, half_number, parity, tile, second, last=False):
        self.h, self.p, self.tile, self.second, self.last = half_number, parity, tile, second, last

    def at(self, per_run, k):
        return self.h * (2 * per_run) + (self.p * per_run + k)


class Sub:

    def __init__(self, batch, c, per_batch):
        self.batch, self.c, self.per_batch = batch, c, per_batch

    def at(self, per_sub, k):
        return self.batch * (self.per_batch * per_sub) + (self.c * per_sub + k)


def after(eng, sem, value):
    if not (isinstance(value, int) and value <= 0):
        eng.wait_ge(sem, value)


def macaron_kernel(nc, x, ffn_w, proj_w, out_w, cols, rows, masks, out):
    fp32, fp32r = mybir.dt.float32, mybir.dt.float32r
    ALU, ACT, AX = mybir.AluOpType, mybir.ActivationFunctionType, mybir.AxisListType

    P = 128
    B, N, D = x.shape
    HEADS = 16
    DH = D // HEADS
    KD = D // P
    HID = 1024
    KH = HID // P
    TT = 512
    NB = TT // P
    TILES = B * N // TT
    TPB = N // TT
    ST = 256
    SB = ST // P
    SUBS = N // ST
    NU, NE = len(UNIQUE), len(OFFSETS)
    ROWS = HEADS * NU
    GROUPS = [list(range(g, min(g + 8, NU))) for g in range(0, NU, 8)]
    FOLD_ROWS = P // HEADS
    SCALE = DH ** -0.5
    FIRST_TWICE = UNIQUE.index(TWICE[0]) * HEADS
    WBLK = 1024
    H_BLOCKS, IN_BLOCKS, OUT_BLOCKS = 2 * KH, 4, 2
    BLOCKS = H_BLOCKS + IN_BLOCKS + OUT_BLOCKS

    valid = [[j for j, o in enumerate(UNIQUE) if o < ST * (c + 1)] for c in range(SUBS)]
    groups_of = [[g for g in range(3) if GROUPS[g][0] in valid[c]] for c in range(SUBS)]
    per_offset = Counts([len(v) for v in valid])
    per_later_offset = Counts([len(v) - 1 for v in valid])
    per_pair = Counts([(len(v) + 1) // 2 for v in valid])
    per_half = Counts([1 if len(g) == 2 else 2 for g in groups_of])

    MM = 2 * KH + KH + KH + NB
    TURN = 2 * KH + KH
    BANKS = MM + 2
    LO = 3 * KH

    x_rows = x.rearrange("b (t n p) d -> (b t) p n d", n=NB, p=P)
    x1 = nc.dram_tensor("x_after_ffn1", (TILES, P, NB, D), fp32)
    x2 = nc.dram_tensor("x_after_attention", (TILES, P, NB, D), fp32)
    out_rows = out.rearrange("b (t n p) d -> (b t) p n d", n=NB, p=P)
    hi_dram = nc.dram_tensor("weights_hi", (H_BLOCKS, P, WBLK), fp32)
    lo_dram = nc.dram_tensor("weights_lo", (BLOCKS, P, WBLK), fp32)

    ctx = ExitStack()
    with ctx:
        def sb(name, shape, dt=fp32):
            return ctx.enter_context(nc.sbuf_tensor(name, shape, dt))

        def sem(name):
            return ctx.enter_context(nc.semaphore(name))

        w_in = sb("w_in", [P, IN_BLOCKS, WBLK], fp32r)
        w_out3 = sb("w_out3", [P, OUT_BLOCKS, WBLK], fp32r)
        wring = sb("wring", [P, 4, WBLK], fp32r)
        wproj = sb("wproj", [P, KD, 4 * D])
        wo = sb("wo", [P, KD, D])
        colv = sb("colv", [P, 40])
        rowv = sb("rowv", [P, 2 * D + NE * HEADS])
        ident = sb("ident", [P, P])
        differ = sb("differ", [P, BLOCKS])
        differ_sum = sb("differ_sum", [P, 1])
        ones = sb("ones", [P, 1])
        flag = sb("flag", [1, 1], mybir.dt.int32)
        sel_in = sb("sel_in", [P, 15 * HEADS])
        sel_out = sb("sel_out", [P, 8, P], fp32r)
        half_neg = sb("half_neg", [P, NB])
        xf = sb("xf", [P, 2, NB, D])
        f_hat = sb("f_hat", [P, 2, D])
        fT_hi = sb("fT_hi", [P, KD, TT], fp32r)
        fT_lo = sb("fT_lo", [P, KD, TT], fp32r)
        h_hi = [sb(f"h_hi{i}", [P, KH, TT], fp32r) for i in range(2)]
        h_lo = [sb(f"h_lo{i}", [P, KH, TT], fp32r) for i in range(2)]
        f_gated = sb("f_gated", [P, 3, TT])
        f_tmp = sb("f_tmp", [P, 2, D])
        f_st = sb("f_st", [P, NB, 6])
        f_mo = sb("f_mo", [P, 5, NB])
        f_mean = sb("f_mean", [P, NB])
        f_var = sb("f_var", [P, NB])
        f_rs = sb("f_rs", [P, NB])
        xa = sb("xa", [P, 2, SB, D])
        a_hat = sb("a_hat", [P, SB, D])
        aT = sb("aT", [P, KD, ST])
        q = sb("q", [P, 2, ST])
        keys = sb("keys", [P, 2, N])
        vals = sb("vals", [P, 2, N])
        gate = sb("gate", [P, 2, ST])
        prod = sb("prod", [P, 4, 2, ST])
        fold = sb("fold", [P, 4, ST])
        sT = sb("sT", [P, 3, ST])
        S = sb("S", [P, SB, NE * HEADS])
        p_hi = sb("p_hi", [P, 3, ST], fp32r)
        p_lo = sb("p_lo", [P, 3, ST], fp32r)
        acc = sb("acc", [P, 2, ST])
        a_tmp = sb("a_tmp", [P, SB, D])
        a_st = sb("a_st", [P, SB, 6])
        a_mo = sb("a_mo", [P, 5, SB])
        a_mean = sb("a_mean", [P, SB])
        a_var = sb("a_var", [P, SB])
        a_rs = sb("a_rs", [P, SB])
        mx = sb("mx", [P, SB, HEADS])
        sm = sb("sm", [P, SB, HEADS])

        fb = [ctx.enter_context(nc.psum_tensor(f"f_bank{i}", [P, 512], fp32)) for i in range(4)]
        ab = [ctx.enter_context(nc.psum_tensor(f"a_bank{i}", [P, 512], fp32)) for i in range(4)]

        def w12(m, w, k):
            o = ((m % 2) * 4 + w * 2 + k) * P
            return w_in[:, m // 2, o:o + P]

        def scale_col(layer, m):
            return colv[:, layer * KH + m:layer * KH + m + 1]

        qkv_bias = [[colv[:, 32 + 2 * w + e:33 + 2 * w + e] for e in range(2)] for w in range(3)]
        gate_bias = [colv[:, 38 + e:39 + e] for e in range(2)]
        s3 = rowv[:, 0:D]
        bout = rowv[:, D:2 * D]
        pos = rowv[:, 2 * D:]

        s_const = sem("s_const")
        s_mask = sem("s_mask")
        s_stage = [sem(f"s_stage{i}") for i in range(2)]
        s_hi = sem("s_hi")
        s_compared = sem("s_compared")
        s_stored = [sem(f"s_stored{i}") for i in range(4)]
        s_counted, s_summed, s_flag = sem("s_counted"), sem("s_summed"), sem("s_flag")
        g_stage = [sem(f"g_stage{i}") for i in range(2)]
        g_hi, g_lo = sem("g_hi"), sem("g_lo")
        g_stored = [sem(f"g_stored{i}") for i in range(2)]
        s_sel = sem("s_sel")
        s_scaled = sem("s_scaled")
        s_neg = sem("s_neg")
        s_stores_seen = sem("s_stores_seen")
        s_ring = [sem(f"s_ring{i}") for i in range(4)]
        f_loaded = [sem(f"f_loaded{i}") for i in range(2)]
        x1_stored, out_stored = sem("x1_stored"), sem("out_stored")
        f_stats, f_summed, f_squared = sem("f_stats"), sem("f_summed"), sem("f_squared")
        f_vareps, f_rstd = sem("f_vareps"), sem("f_rstd")
        f_norm, f_turned, f_thi, f_tlo = sem("f_norm"), sem("f_turned"), sem("f_thi"), sem("f_tlo")
        f_mm, f_silu, f_prod, f_phi = sem("f_mm"), sem("f_silu"), sem("f_prod"), sem("f_phi")
        f_gelu, f_lo, f_outs, f_x = sem("f_gelu"), sem("f_lo"), sem("f_outs"), sem("f_x")
        a_loaded = [sem(f"a_loaded{i}") for i in range(2)]
        a_stored = [sem(f"a_stored{i}") for i in range(2)]
        a_stats, a_summed, a_squared = sem("a_stats"), sem("a_summed"), sem("a_squared")
        a_vareps, a_rstd = sem("a_vareps"), sem("a_rstd")
        a_norm, a_turned, a_xT = sem("a_norm"), sem("a_turned"), sem("a_xT")
        a_proj, a_qkv, a_gexp = sem("a_proj"), sem("a_qkv"), sem("a_gexp")
        a_gone, a_gate = sem("a_gone"), sem("a_gate")
        a_qk, a_fold, a_scored = sem("a_qk"), sem("a_fold"), sem("a_scored")
        a_scopied, a_sturned, a_biased = sem("a_scopied"), sem("a_sturned"), sem("a_biased")
        a_max, a_less, a_exp, a_sum = sem("a_max"), sem("a_less"), sem("a_exp"), sem("a_sum")
        a_recip, a_probs, a_pturned = sem("a_recip"), sem("a_probs"), sem("a_pturned")
        a_phi, a_plo, a_spread_done = sem("a_phi"), sem("a_plo"), sem("a_spread_done")
        a_pv, a_acc, a_z = sem("a_pv"), sem("a_acc"), sem("a_z")
        a_wo, a_otmp, a_x = sem("a_wo"), sem("a_otmp"), sem("a_x")

        block = ctx.enter_context(nc.Block())

        FFN_TIME = KH * 1.7 + 2 * KH * 3.4 + 6.8

        def schedule(eng, do, at="end"):

            def ffn_steps(r, following, now):
                steps = []

                def add(time, name, *args):
                    nonlocal now
                    place = {"start": now, "ahead": now - 7, "end": now + time}[at]
                    steps.append((place, name, args))
                    now += time

                for m in range(KH + 1):
                    add(1.7 if m < KH else 0.0, "f_in", r, m)
                inside = {(0, 3): ("f_load", ()), (0, 5): ("f_norm", ()),
                          (1, 0): ("f_turn", (0, r)), (1, 1): ("f_turn", (1, r))}
                for layer in range(2):
                    for m in range(KH):
                        add(3.4, "f_hidden", r, layer, m)
                        if following is not None and (layer, m) in inside:
                            name, args = inside[layer, m]
                            steps.append((now, name, (following, *args)))
                add(6.8, "f_out", r)
                steps.append((now, "f_store", (r,)))
                return steps

            def attention_steps(a, tile, u, start, span):
                v = valid[a.c]
                steps = [(-6, "a_load", (tile, u)), (-2, "a_norm", (a,)), (4, "a_turn", (a,)), (6, "a_project", (a,)),
                         (9, "a_gate", (a,))]
                for k in range(len(v)):
                    steps.append((9 + 0.9 * k, "a_score", (a, k)))
                    steps.append((12 + 0.9 * k, "a_sum_heads", (a, k)))
                now = 12 + 0.9 * len(v)
                steps += [(now + 1, "a_scopy", (a,)), (now + 2, "a_sturn", (a,)), (now + 4, "a_softmax", (a,)),
                          (now + 12, "a_pturn", (a,)), (now + 13, "a_pcut", (a,))]
                now += 15
                for k in range(len(v)):
                    if k % 2 == 0:
                        steps.append((now + 1.1 * k, "a_spread", (a, k // 2)))
                    steps.append((now + 1.5 + 1.1 * k, "a_weigh", (a, k)))
                now += 1.1 * len(v) + 3
                steps += [(now, "a_gated", (a,)), (now + 3, "a_wout", (a,)), (now + 4, "a_residual", (a, u)),
                          (now + 6, "a_store", (a, tile, u))]
                return [(start + t * span / (now + 6), name, args) for t, name, args in steps]

            def together(runs, tiles):
                steps = []
                for i, (r, following) in enumerate(zip(runs, runs[1:])):
                    steps += ffn_steps(r, following, i * FFN_TIME)
                for batch, c, tile, start, time in tiles:
                    for u in range(2):
                        steps += attention_steps(Sub(batch, c + u, SUBS), tile, u, start + time / 2 * u, time / 2)
                for _, name, args in sorted(steps, key=lambda s: s[0]):
                    if name in do:
                        do[name](*args)

            def ffn1(tile):
                return Ffn(tile - 1, 0, tile, False)

            def ffn2(tile):
                return Ffn(tile + 1, 1, tile, True)

            head = [Ffn(0, 0, 0, False), Ffn(0, 1, 1, False), ffn1(2)]
            for name, args in (("f_load", ()), ("f_norm", ()), ("f_turn", (0, None)), ("f_turn", (1, None))):
                if name in do:
                    do[name](head[0], *args)
            together(head, [(0, 0, 0, FFN_TIME + 4, FFN_TIME - 5)])

            with eng.Fori(1, TILES // 2 - 1) as k:
                for odd in range(2):
                    i = k * 2 + odd
                    together([ffn1(i), ffn2(i - 2), ffn1(i + 1)],
                             [(k - 1 + odd, 2 - 2 * odd, i - 1, 1, 2 * FFN_TIME - 3)])

            n = TILES
            tail = [ffn1(n - 2), ffn2(n - 4), ffn1(n - 1), ffn2(n - 3), Ffn(n - 1, 0, n - 2, True),
                    Ffn(n - 1, 1, n - 1, True, last=True), None]
            together(tail, [(B - 2, SUBS - 2, n - 3, 1, 114), (B - 1, 0, n - 2, 116, 112),
                            (B - 1, SUBS - 2, n - 1, 231, 94)])

        class Ring:

            def __init__(self, general):
                blocks = []
                for j in range(IN_BLOCKS if general else 0):
                    blocks.append(("lo", H_BLOCKS + j, ("f_in", 2 * j), 4 * (j + 1)))
                for layer in range(2):
                    for m in range(KH):
                        for source in ("hi", "lo")[:2 if general else 1]:
                            n = 2 * KH + layer * KH + m + 1
                            blocks.append((source, layer * KH + m, ("f_hidden", layer, m), n))
                for j in range(OUT_BLOCKS if general else 0):
                    blocks.append(("lo", H_BLOCKS + IN_BLOCKS + j, ("f_out",), MM))
                self.blocks, self.slots = blocks, 2 if general else 4
                assert len(blocks) % self.slots == 0

            def of_step(self, *step):
                return [i for i, b in enumerate(self.blocks) if b[2] == step]

            def filled(self, r, i):
                return r.at(16 * (len(self.blocks) // self.slots), 16 * (i // self.slots + 1))

            def freed(self, r, i):
                return r.at(MM, self.blocks[i - self.slots][3] if i >= self.slots else 0)

        def f_bank(r, n):
            return fb[(r.p * BANKS + n) % 4]

        def turn_bank(r, bp):
            return fb[((1 - r.p) * BANKS + TURN + bp) % 4]

        def hidden_use(layer, m):
            return 2 * KH + m if layer == 0 else TURN + 2 + m

        @block.sync
        def _(sp):
            sp.dma_start(colv[:, :], cols).then_inc(s_const, 16)
            sp.dma_start(rowv[:, :], rows.partition_broadcast(P)).then_inc(s_const, 16)
            sp.dma_start(ident[:, :], masks[:, 0:P]).then_inc(s_const, 16)
            sp.dma_start(sel_in[:, :], masks[:, P:P + 15 * HEADS]).then_inc(s_const, 16)
            sp.dma_start(wproj[:, :, :], proj_w).then_inc(s_const, 16)
            sp.dma_start(wo[:, :, :], out_w).then_inc(s_const, 16)
            sp.dma_start(prod[:, :, :, :].rearrange("p a e n -> p (a e n)")[:, 0:8 * P],
                         masks[:, P + 15 * HEADS:]).then_inc(s_mask, 16)

            def stage(i, slot):
                sp.dma_start(xf[:, slot, :, :].rearrange("p n d -> p (n d)"), ffn_w[i, :, :])\
                    .then_inc(s_stage[slot], 16)

            stage(0, 0)
            stage(1, 1)
            with sp.Fori(0, H_BLOCKS // 4) as it:
                for s in range(4):
                    sp.wait_ge(s_compared, it * 4 + (s + 1))
                    sp.dma_start(hi_dram[it * 4 + s, :, :], h_hi[0][:, 2 * s:2 * s + 2, :].bitcast(fp32))\
                        .then_inc(s_stored[s], 16)
                    stage(it * 4 + s + 2, s % 2)
            for i in range(H_BLOCKS, BLOCKS - 2):
                sp.wait_ge(s_compared, i + 1)
                stage(i + 2, i % 2)
            for s in range(4):
                sp.wait_ge(s_stored[s], 16 * (H_BLOCKS // 4))
            sp.wait_ge(s_flag, 1)
            has_lo = sp.value_load(flag[0:1, 0:1])

            def lo_parts():
                def load(i, slot):
                    sp.dma_start(xf[:, slot, :, :].rearrange("p n d -> p (n d)"), ffn_w[i, :, :])\
                        .then_inc(g_stage[slot], 16)

                def store(i, slot):
                    sp.dma_start(lo_dram[i, :, :], h_lo[0][:, 2 * slot:2 * slot + 2, :].bitcast(fp32))\
                        .then_inc(g_stored[slot], 16)

                load(0, 0)
                load(1, 1)
                with sp.Fori(0, BLOCKS // 2 - 1) as it:
                    for slot in range(2):
                        sp.wait_ge(g_lo, it * 2 + (slot + 1))
                        store(it * 2 + slot, slot)
                        load(it * 2 + slot + 2, slot)
                for slot in range(2):
                    sp.wait_ge(g_lo, BLOCKS - 1 + slot)
                    store(BLOCKS - 2 + slot, slot)
                for slot in range(2):
                    sp.wait_ge(g_stored[slot], 16 * (BLOCKS // 2))

            def alone():
                sp.sem_inc(s_stores_seen, 1)

            def f_load(r):
                src = x2[r.tile, :, :, :] if r.second else x_rows[r.tile, :, :, :]
                sp.dma_start(xf[:, r.p, :, :], src).then_inc(f_loaded[r.p], 16)

            def f_store(r):
                sp.wait_ge(f_x, r.at(NB, NB))
                dst, stored = (out_rows, out_stored) if r.second else (x1, x1_stored)
                sp.dma_start(dst[r.tile, :, :, :], xf[:, r.p, :, :]).then_inc(stored, 16)
                sp.wait_ge(stored, r.tile * 16 + 16)
                alone()

            def a_load(tile, u):
                sp.dma_start(xa[:, u, :, :], x1[tile, :, u * SB:(u + 1) * SB, :]).then_inc(a_loaded[u], 16)

            def a_store(a, tile, u):
                sp.wait_ge(a_x, a.at(1, 1))
                sp.dma_start(x2[tile, :, u * SB:(u + 1) * SB, :], xa[:, u, :, :]).then_inc(a_stored[u], 16)
                sp.wait_ge(a_stored[u], tile * 16 + 16)
                alone()

            def run(general):
                ring = Ring(general)

                def fill(r, *step):
                    for i in ring.of_step(*step):
                        source, blk, _, _ = ring.blocks[i]
                        after(sp, f_mm, ring.freed(r, i))
                        sp.dma_start(wring[:, i % ring.slots, :].bitcast(fp32),
                                     (hi_dram if source == "hi" else lo_dram)[blk, :, :])\
                            .then_inc(s_ring[i % ring.slots], 16)

                schedule(sp, {
                    "f_load": f_load, "f_store": f_store, "a_load": a_load, "a_store": a_store,
                    "f_in": lambda r, m: fill(r, "f_in", m),
                    "f_hidden": lambda r, layer, m: fill(r, "f_hidden", layer, m),
                    "f_out": lambda r: fill(r, "f_out"),
                }, at="ahead")

            with sp.If(has_lo != 0):
                lo_parts()
                run(True)
            with sp.Else():
                run(False)

        @block.gpsimd
        def _(pool):
            pool.memset(half_neg[:, :], -0.5).then_inc(s_neg, 1)
            pool.wait_ge(s_neg, 1)

            def f_norm_(r):
                pool.wait_ge(f_vareps, r.at(1, 1))
                pool.tensor_tensor(f_rs[:, :], f_var[:, :], half_neg[:, :], ALU.pow).then_inc(f_rstd, 1)

            def a_norm_(a):
                pool.wait_ge(a_vareps, a.at(1, 1))
                pool.tensor_tensor(a_rs[:, :], a_var[:, :], half_neg[:, 0:SB], ALU.pow).then_inc(a_rstd, 1)

            def a_score(a, k):
                lo = max(0, UNIQUE[valid[a.c][k]] - ST * a.c)
                pool.wait_ge(a_qk, per_offset.at(a, k + 1))
                if k >= 4:
                    pool.wait_ge(a_scored, per_offset.at(a, k - 3))
                else:
                    after(pool, a_scored, per_offset.at(a, 0))
                last = pool.tensor_tensor(fold[:, k % 4, lo:ST], prod[:, k % 4, 0, lo:ST],
                                          prod[:, k % 4, 1, lo:ST], ALU.add)
                if lo and valid[a.c][k] % 8 == 0:
                    last = pool.memset(fold[:, k % 4, 0:lo], 0.0)
                last.then_inc(a_fold, 1)

            def a_weigh(a, k):
                if k == 0:
                    return
                lo = max(0, UNIQUE[valid[a.c][k]] - ST * a.c)
                pool.wait_ge(a_pv, per_later_offset.at(a, k))
                pool.wait_ge(a_acc, per_offset.at(a, k))
                pool.tensor_tensor(acc[:, :, lo:ST], acc[:, :, lo:ST], prod[:, k % 4, :, lo:ST], ALU.add)\
                    .then_inc(a_acc, 1)

            schedule(pool, {"f_norm": f_norm_, "a_norm": a_norm_, "a_score": a_score, "a_weigh": a_weigh})

        @block.scalar
        def _(act):
            act.wait_ge(s_mask, 16)
            act.activation(sel_out[:, :, :].rearrange("p j f -> p (j f)"),
                           prod[:, :, :, :].rearrange("p a e n -> p (a e n)")[:, 0:8 * P], ACT.Copy)\
                .then_inc(s_sel, 1)

            def cut_hi(s, stage_value, dst):
                act.wait_ge(s_stage[s % 2], stage_value)
                act.activation(dst, xf[:, s % 2, :, :].rearrange("p n d -> p (n d)"), ACT.Copy).then_inc(s_hi, 1)

            for s in range(4):
                cut_hi(s, 16 * (s // 2 + 1), h_hi[0][:, 2 * s:2 * s + 2, :].rearrange("p a n -> p (a n)"))
            with act.Fori(1, H_BLOCKS // 4) as it:
                for s in range(4):
                    act.wait_ge(s_stored[s], it * 16)
                    cut_hi(s, it * 32 + 16 * (s // 2 + 1),
                           h_hi[0][:, 2 * s:2 * s + 2, :].rearrange("p a n -> p (a n)"))
            for i in range(H_BLOCKS, BLOCKS):
                j = i - H_BLOCKS
                dst = w_in[:, j, :] if j < IN_BLOCKS else w_out3[:, j - IN_BLOCKS, :]
                cut_hi(i % 4, 16 * (i // 2 + 1), dst)
            act.wait_ge(s_scaled, 3)

            def f_turn(r, bp, before):
                act.wait_ge(f_turned, r.at(2, bp + 1))
                act.activation(fT_hi[:, :, bp * ST:(bp + 1) * ST],
                               turn_bank(r, bp)[:, :].rearrange("p (k n) -> p k n", k=KD), ACT.Copy)\
                    .then_inc(f_thi, 1)

            def f_in(r, m):
                if m < KH:
                    bank = f_bank(r, 2 * m)
                    act.wait_ge(f_mm, r.at(MM, 2 * m + 1))
                    if m >= 3:
                        act.wait_ge(f_lo, r.at(LO, m - 2))
                    act.activation(f_gated[:, m % 3, :], bank[:, :], ACT.Silu, scale=scale_col(0, m)).then_inc(f_silu, 1)
                if m > 0:
                    act.wait_ge(f_prod, r.at(KH, m))
                    act.activation(h_hi[r.p][:, m - 1, :], f_gated[:, (m - 1) % 3, :], ACT.Copy).then_inc(f_phi, 1)

            def f_hidden(r, layer, m):
                n = 2 * KH + layer * KH + m
                bank, dst = f_bank(r, hidden_use(layer, m)), h_hi[(r.p + 1 + layer) % 2]
                act.wait_ge(f_mm, r.at(MM, n + 1))
                act.activation(dst[:, m, :], bank[:, :], ACT.Gelu, scale=scale_col(2 + layer, m))
                act.activation(bank[:, :], bank[:, :], ACT.Gelu, scale=scale_col(2 + layer, m)).then_inc(f_gelu, 1)

            def a_turn(a):
                act.wait_ge(a_turned, a.at(1, 1))
                act.activation(aT[:, :, :].rearrange("p k n -> p (k n)"), ab[0][:, :], ACT.Copy).then_inc(a_xT, 1)

            def a_project(a):
                s0 = ST * a.c
                for w, dst in enumerate((q[:, :, :], keys[:, :, s0:s0 + ST], vals[:, :, s0:s0 + ST])):
                    act.wait_ge(a_proj, a.at(4, w + 1))
                    for e in range(2):
                        last = act.activation(dst[:, e, :], ab[1 + w][:, e * ST:(e + 1) * ST], ACT.Identity,
                                              bias=qkv_bias[w][e], scale=SCALE if w == 0 else 1.0)
                    last.then_inc(a_qkv, 1)
                act.wait_ge(a_proj, a.at(4, 4))
                for e in range(2):
                    last = act.activation(gate[:, e, :], ab[0][:, e * ST:(e + 1) * ST], ACT.Exp,
                                          bias=gate_bias[e], scale=-1.0)
                last.then_inc(a_gexp, 1)

            def a_scopy(a):
                v, gs = valid[a.c], groups_of[a.c]
                act.wait_ge(a_scored, per_offset.at(a, 16))
                act.activation(sT[:, 0:2, :].rearrange("p g n -> p (g n)"), ab[1][:, :], ACT.Copy).then_inc(a_scopied, 1)
                if len(gs) > 2:
                    act.wait_ge(a_scored, per_offset.at(a, len(v)))
                    act.activation(sT[0:64, 2, :], ab[2][0:64, 0:ST], ACT.Copy).then_inc(a_scopied, 1)

            def a_softmax(a):
                act.wait_ge(a_less, a.at(1, 1))
                act.activation(S[:, :, :], S[:, :, :], ACT.Exp).then_inc(a_exp, 1)

            def a_pcut(a):
                act.wait_ge(a_pturned, per_half.at(a, 1))
                act.activation(p_hi[:, 0:2, :].rearrange("p g n -> p (g n)"), ab[1][:, :], ACT.Copy).then_inc(a_phi, 1)
                if len(groups_of[a.c]) > 2:
                    act.wait_ge(a_pturned, per_half.at(a, 2))
                    act.activation(p_hi[0:64, 2, :], ab[2][0:64, 0:ST], ACT.Copy).then_inc(a_phi, 1)

            schedule(act, {"f_turn": f_turn, "f_in": f_in, "f_hidden": f_hidden, "a_turn": a_turn,
                           "a_project": a_project, "a_scopy": a_scopy, "a_softmax": a_softmax, "a_pcut": a_pcut})

        @block.vector
        def _(dve):
            dve.wait_ge(s_const, 16 * 6)
            dve.tensor_scalar(s3, s3, 0.5, None, ALU.mult).then_inc(s_scaled, 1)
            dve.tensor_scalar(colv[:, 32:34], colv[:, 32:34], SCALE, None, ALU.mult).then_inc(s_scaled, 1)
            dve.tensor_scalar(colv[:, 38:40], colv[:, 38:40], -1.0, None, ALU.mult).then_inc(s_scaled, 1)

            def compare(i, s, hi_value, hi, count):
                dve.wait_ge(s_hi, hi_value)
                dve.scalar_tensor_tensor(h_lo[0][:, 2 * s:2 * s + 2, :].rearrange("p a n -> p (a n)"),
                                         xf[:, s % 2, :, :].rearrange("p n d -> p (n d)"), 1.0, hi.bitcast(fp32),
                                         ALU.mult, ALU.not_equal, accum_out=count).then_inc(s_compared, 1)

            def h_slot(s):
                return h_hi[0][:, 2 * s:2 * s + 2, :].rearrange("p a n -> p (a n)")

            with dve.Fori(0, H_BLOCKS // 4) as it:
                for s in range(4):
                    compare(it * 4 + s, s, it * 4 + (s + 1), h_slot(s), differ[:, bass.ds(it * 4 + s, 1)])
            for i in range(H_BLOCKS, BLOCKS):
                j = i - H_BLOCKS
                hi = w_in[:, j, :] if j < IN_BLOCKS else w_out3[:, j - IN_BLOCKS, :]
                compare(i, i % 4, i + 1, hi, differ[:, i:i + 1])
            dve.wait_ge(s_scaled, 3)
            dve.wait_ge(s_compared, BLOCKS)
            dve.tensor_reduce(differ_sum[:, :], differ[:, :], AX.X, ALU.add)
            dve.memset(ones[:, :], 1.0).then_inc(s_summed, 1)
            dve.wait_ge(s_counted, 1)
            dve.tensor_scalar(flag[:, :], ab[0][0:1, 0:1], 1.0, None, ALU.min).then_inc(s_flag, 1)
            dve.wait_ge(s_flag, 1)
            has_lo = dve.value_load(flag[0:1, 0:1])
            with dve.If(has_lo != 0):
                def lo_part(it, s, slot_used):
                    dve.wait_ge(g_stage[s], it * 16 + 16)
                    dve.tensor_copy(h_slot(s), xf[:, s, :, :].rearrange("p n d -> p (n d)")).then_inc(g_hi, 1)
                    dve.wait_ge(g_hi, it * 2 + (s + 1))
                    if slot_used:
                        dve.wait_ge(g_stored[s], it * 16)
                    dve.tensor_tensor(h_lo[0][:, 2 * s:2 * s + 2, :].rearrange("p a n -> p (a n)"),
                                      xf[:, s, :, :].rearrange("p n d -> p (n d)"), h_slot(s).bitcast(fp32),
                                      ALU.subtract).then_inc(g_lo, 1)

                for s in range(2):
                    lo_part(0, s, False)
                with dve.Fori(1, BLOCKS // 2) as it:
                    for s in range(2):
                        lo_part(it, s, True)

            def moments(run, st, mo, mean, var, stats, summed, squared, vareps):
                even, odd = (1, 2), (4, 5)
                dve.wait_ge(stats, run.at(1, 1))
                dve.tensor_tensor(mo[:, 0, :], st[:, :, even[0]], st[:, :, odd[0]], ALU.add)
                dve.tensor_tensor(mo[:, 1, :], st[:, :, even[0]], st[:, :, odd[0]], ALU.subtract)
                dve.tensor_tensor(mo[:, 2, :], st[:, :, even[1]], st[:, :, odd[1]], ALU.add).then_inc(summed, 1)
                dve.wait_ge(summed, run.at(1, 1))
                dve.tensor_scalar(mean[:, :], mo[:, 0, :], 0.5, None, ALU.mult)
                dve.tensor_tensor(mo[:, 3, :], mo[:, 1, :], mo[:, 1, :], ALU.mult)
                dve.tensor_scalar(mo[:, 4, :], mo[:, 2, :], 1.0 / D, EPS, ALU.mult, ALU.add).then_inc(squared, 1)
                dve.wait_ge(squared, run.at(1, 1))
                dve.scalar_tensor_tensor(var[:, :], mo[:, 3, :], 0.25, mo[:, 4, :], ALU.mult, ALU.add)\
                    .then_inc(vareps, 1)

            def f_norm_(r):
                dve.wait_ge(f_loaded[r.p], r.h * 16 + 16 + 0)
                for n in range(NB):
                    last = dve.bn_stats(f_st[:, n, :], xf[:, r.p, n, :])
                last.then_inc(f_stats, 1)
                moments(r, f_st, f_mo, f_mean, f_var, f_stats, f_summed, f_squared, f_vareps)
                dve.wait_ge(f_rstd, r.at(1, 1))
                f_scale(r, 0)

            def f_scale(r, bp):
                for n in range(2):
                    i = 2 * bp + n
                    last = dve.tensor_scalar(f_hat[:, n, :], xf[:, r.p, i, :], f_mean[:, i:i + 1],
                                             f_rs[:, i:i + 1], ALU.subtract, ALU.mult)
                last.then_inc(f_norm, 1)

            def f_turn(r, bp, before):
                if bp == 0:
                    dve.wait_ge(f_turned, r.at(2, 1))
                    f_scale(r, 1)
                dve.wait_ge(f_thi, r.at(2, bp + 1))
                part = slice(bp * ST, (bp + 1) * ST)
                dve.tensor_tensor(fT_lo[:, :, part], turn_bank(r, bp)[:, :].rearrange("p (k n) -> p k n", k=KD),
                                  fT_hi[:, :, part].bitcast(fp32), ALU.subtract).then_inc(f_tlo, 1)

            def f_in(r, m):
                if m < KH:
                    g, u = f_gated[:, m % 3, :], f_bank(r, 2 * m + 1)
                    dve.wait_ge(f_silu, r.at(KH, m + 1))
                    dve.wait_ge(f_mm, r.at(MM, 2 * m + 2))
                    dve.scalar_tensor_tensor(g, u[:, :], scale_col(1, m), g, ALU.mult, ALU.mult)\
                        .then_inc(f_prod, 1)
                if m > 0:
                    dve.wait_ge(f_phi, r.at(KH, m))
                    dve.tensor_tensor(h_lo[r.p][:, m - 1, :], f_gated[:, (m - 1) % 3, :],
                                      h_hi[r.p][:, m - 1, :].bitcast(fp32), ALU.subtract).then_inc(f_lo, 1)

            def f_hidden(r, layer, m):
                bank = f_bank(r, hidden_use(layer, m))
                i = (r.p + 1 + layer) % 2
                dve.wait_ge(f_gelu, r.at(2 * KH, layer * KH + m + 1))
                dve.tensor_tensor(h_lo[i][:, m, :], bank[:, :], h_hi[i][:, m, :].bitcast(fp32),
                                  ALU.subtract).then_inc(f_lo, 1)

            def f_out(r):
                for n in range(NB):
                    dve.wait_ge(f_mm, r.at(MM, 4 * KH + n + 1))
                    after(dve, f_x, r.at(NB, n - 1))
                    dve.tensor_tensor(f_tmp[:, n % 2, :], f_bank(r, 4 * KH + 2 + n)[:, 0:D], s3, ALU.mult)\
                        .then_inc(f_outs, 1)
                    dve.wait_ge(f_outs, r.at(NB, n + 1))
                    dve.tensor_tensor(xf[:, r.p, n, :], xf[:, r.p, n, :], f_tmp[:, n % 2, :], ALU.add)\
                        .then_inc(f_x, 1)

            def a_norm_(a):
                u = a.c % 2
                dve.wait_ge(a_loaded[u], a.batch * (16 * TPB) + 16 * (a.c // 2 + 1))
                for n in range(SB):
                    last = dve.bn_stats(a_st[:, n, :], xa[:, u, n, :])
                last.then_inc(a_stats, 1)
                moments(a, a_st, a_mo, a_mean, a_var, a_stats, a_summed, a_squared, a_vareps)
                dve.wait_ge(a_rstd, a.at(1, 1))
                for n in range(SB):
                    last = dve.tensor_scalar(a_hat[:, n, :], xa[:, u, n, :], a_mean[:, n:n + 1],
                                             a_rs[:, n:n + 1], ALU.subtract, ALU.mult)
                last.then_inc(a_norm, 1)

            def a_gate_(a):
                dve.wait_ge(a_gexp, a.at(1, 1))
                dve.tensor_scalar(gate[:, :, :], gate[:, :, :], 1.0, None, ALU.add).then_inc(a_gone, 1)
                dve.wait_ge(a_gone, a.at(1, 1))
                dve.reciprocal(gate[:, :, :], gate[:, :, :]).then_inc(a_gate, 1)

            def shifted(a, k):
                s0, o = ST * a.c, UNIQUE[valid[a.c][k]]
                lo = max(0, o - s0)
                return lo, slice(s0 - o + lo, s0 - o + ST)

            def a_score(a, k):
                lo, back = shifted(a, k)
                if k == 0:
                    dve.wait_ge(a_qkv, a.at(3, 3))
                if k >= 4:
                    dve.wait_ge(a_fold, per_offset.at(a, k - 3))
                dve.tensor_tensor(prod[:, k % 4, :, lo:ST], q[:, :, lo:ST], keys[:, :, back], ALU.mult)\
                    .then_inc(a_qk, 1)

            def a_softmax(a):
                gs = groups_of[a.c]
                for n in range(SB):
                    bank = ab[3] if n == 0 else ab[0]
                    dve.wait_ge(a_sturned, a.at(SB, n + 1))
                    w = ROWS if len(gs) > 2 else 2 * P
                    dve.tensor_tensor(S[:, n, 0:w], bank[:, 0:w], pos[:, 0:w], ALU.add)
                    if w < ROWS:
                        dve.tensor_copy(S[:, n, w:ROWS], pos[:, w:ROWS])
                    dve.tensor_tensor(S[:, n, ROWS:], bank[:, FIRST_TWICE:FIRST_TWICE + len(TWICE) * HEADS],
                                      pos[:, ROWS:], ALU.add).then_inc(a_biased, 1)
                by_head = S[:, :, :].rearrange("p n (e h) -> p n h e", h=HEADS)
                by_entry = S[:, :, :].rearrange("p n (e h) -> p n e h", h=HEADS)
                dve.wait_ge(a_biased, a.at(SB, SB))
                dve.tensor_reduce(mx[:, :, :], by_head, AX.X, ALU.max).then_inc(a_max, 1)
                dve.wait_ge(a_max, a.at(1, 1))
                dve.tensor_tensor(by_entry, by_entry, mx[:, :, :].unsqueeze(2).to_broadcast([P, SB, NE, HEADS]),
                                  ALU.subtract).then_inc(a_less, 1)
                dve.wait_ge(a_exp, a.at(1, 1))
                dve.tensor_reduce(sm[:, :, :], by_head, AX.X, ALU.add).then_inc(a_sum, 1)
                dve.wait_ge(a_sum, a.at(1, 1))
                both = S[:, :, FIRST_TWICE:FIRST_TWICE + len(TWICE) * HEADS]
                dve.tensor_tensor(both, both, S[:, :, ROWS:], ALU.add)
                dve.reciprocal(sm[:, :, :], sm[:, :, :]).then_inc(a_recip, 1)
                dve.wait_ge(a_recip, a.at(1, 1))
                probs = S[:, :, 0:ROWS].rearrange("p n (e h) -> p n e h", h=HEADS)
                dve.tensor_tensor(probs, probs, sm[:, :, :].unsqueeze(2).to_broadcast([P, SB, NU, HEADS]),
                                  ALU.mult).then_inc(a_probs, 1)

            def a_pcut(a):
                gs = groups_of[a.c]
                dve.wait_ge(a_phi, per_half.at(a, 1))
                dve.tensor_tensor(p_lo[:, 0:2, :].rearrange("p g n -> p (g n)"), ab[1][:, :],
                                  p_hi[:, 0:2, :].rearrange("p g n -> p (g n)").bitcast(fp32), ALU.subtract)\
                    .then_inc(a_plo, 1)
                if len(gs) > 2:
                    dve.wait_ge(a_phi, per_half.at(a, 2))
                    dve.tensor_tensor(p_lo[0:64, 2, :], ab[2][0:64, 0:ST], p_hi[0:64, 2, :].bitcast(fp32),
                                      ALU.subtract).then_inc(a_plo, 1)

            def a_weigh(a, k):
                lo, back = shifted(a, k)
                bank = ab[(3, 0, 1)[k // 2 % 3]]
                if k % 2 == 0:
                    dve.wait_ge(a_spread_done, per_pair.at(a, k // 2 + 1))
                if k >= 5:
                    dve.wait_ge(a_acc, per_offset.at(a, k - 3))
                spread = bank[:, (k % 2) * ST + lo:(k % 2 + 1) * ST].unsqueeze(1).to_broadcast([P, 2, ST - lo])
                dst = acc[:, :, :] if k == 0 else prod[:, k % 4, :, lo:ST]
                dve.tensor_tensor(dst, vals[:, :, back], spread, ALU.mult).then_inc(a_acc if k == 0 else a_pv, 1)

            def a_gated(a):
                dve.wait_ge(a_acc, per_offset.at(a, len(valid[a.c])))
                dve.tensor_tensor(acc[:, :, :], acc[:, :, :], gate[:, :, :], ALU.mult).then_inc(a_z, 1)

            def a_residual(a, u):
                rows_ = xa[:, u, :, :]
                dve.wait_ge(a_wo, a.at(1, 1))
                dve.tensor_tensor(a_tmp[:, :, :], ab[2][:, :].rearrange("p (n d) -> p n d", n=SB), rows_,
                                  ALU.add).then_inc(a_otmp, 1)
                dve.wait_ge(a_otmp, a.at(1, 1))
                dve.tensor_tensor(rows_, a_tmp[:, :, :], bout.unsqueeze(1).to_broadcast([P, SB, D]), ALU.add)\
                    .then_inc(a_x, 1)

            schedule(dve, {"f_norm": f_norm_, "f_turn": f_turn, "f_in": f_in, "f_hidden": f_hidden, "f_out": f_out,
                           "a_norm": a_norm_, "a_gate": a_gate_, "a_score": a_score,
                           "a_softmax": a_softmax, "a_pcut": a_pcut, "a_weigh": a_weigh, "a_gated": a_gated,
                           "a_residual": a_residual})

        @block.tensor
        def _(pe):
            pe.wait_ge(s_const, 16 * 6)
            pe.wait_ge(s_sel, 1)
            pe.wait_ge(s_summed, 1)
            pe.matmul(ab[0][0:1, 0:1], differ_sum[:, :], ones[:, :], start=True, stop=True).then_inc(s_counted, 1)
            pe.wait_ge(s_flag, 1)
            has_lo = pe.value_load(flag[0:1, 0:1])

            def f_turn(r, bp, before):
                if before is not None:
                    pe.wait_ge(f_lo, before.at(LO, KH + 4 + bp + 1))
                pe.wait_ge(f_norm, r.at(2, bp + 1))
                for kc in range(KD):
                    for n in range(2):
                        last = pe.transpose(turn_bank(r, bp)[:, kc * ST + n * P:kc * ST + (n + 1) * P],
                                            f_hat[:, n, kc * P:(kc + 1) * P], ident[:, :])
                last.then_inc(f_turned, 1)

            def run_in(r, m, ring, general):
                if m == KH:
                    return
                if general:
                    (i,) = ring.of_step("f_in", m - m % 2)
                    pe.wait_ge(s_ring[i % ring.slots], ring.filled(r, i))
                if m == 0:
                    pe.wait_ge(f_tlo, r.at(2, 2))
                for w in range(2):
                    n = 2 * m + w
                    bank = f_bank(r, n)
                    if n < 4:
                        after(pe, f_outs, r.at(NB, n - 3))
                    else:
                        pe.wait_ge(f_prod if w else f_silu, r.at(KH, m - 1))
                    for k in range(KD):
                        pe.matmul(bank[:, :], w12(m, w, k), fT_hi[:, k, :], start=(k == 0), stop=False)
                        last = pe.matmul(bank[:, :], w12(m, w, k), fT_lo[:, k, :], start=False,
                                         stop=(not general and k == KD - 1))
                    for k in range(KD if general else 0):
                        o = ((m % 2) * 4 + w * 2 + k) * P
                        last = pe.matmul(bank[:, :], wring[:, i % ring.slots, o:o + P], fT_hi[:, k, :],
                                         start=False, stop=(k == KD - 1))
                    last.then_inc(f_mm, 1)

            def run_hidden(r, layer, m, ring, general):
                src = (r.p + layer) % 2
                bank = f_bank(r, hidden_use(layer, m))
                blocks = ring.of_step("f_hidden", layer, m)
                if m >= 4:
                    pe.wait_ge(f_lo, r.at(LO, (1 + layer) * KH + m - 3))
                elif layer == 0:
                    pe.wait_ge(f_prod if m % 2 else f_silu, r.at(KH, KH - 2 + m // 2 + 1))
                elif m < 2:
                    pe.wait_ge(f_lo, r.at(LO, 2 * KH - 2 + m + 1))
                elif not r.last:
                    pe.wait_ge(f_tlo, r.at(2, 2 + m - 1))
                for i in blocks:
                    pe.wait_ge(s_ring[i % ring.slots], ring.filled(r, i))
                for k in range(KH):
                    if m == 0:
                        pe.wait_ge(f_lo, r.at(LO, layer * KH + k + 1))
                    hi = wring[:, blocks[0] % ring.slots, k * P:(k + 1) * P]
                    pe.matmul(bank[:, :], hi, h_hi[src][:, k, :], start=(k == 0), stop=False)
                    last = pe.matmul(bank[:, :], hi, h_lo[src][:, k, :], start=False,
                                     stop=(not general and k == KH - 1))
                for k in range(KH if general else 0):
                    lo = wring[:, blocks[1] % ring.slots, k * P:(k + 1) * P]
                    last = pe.matmul(bank[:, :], lo, h_hi[src][:, k, :], start=False, stop=(k == KH - 1))
                last.then_inc(f_mm, 1)

            def run_out(r, ring, general):
                blocks = ring.of_step("f_out")
                for i in blocks:
                    pe.wait_ge(s_ring[i % ring.slots], ring.filled(r, i))

                def part(n, k):
                    to = f_bank(r, 4 * KH + 2 + n)[:, 0:D]
                    t = slice(n * P, (n + 1) * P)
                    w = w_out3[:, k // 4, (k % 4) * D:(k % 4 + 1) * D]
                    pe.matmul(to, h_hi[r.p][:, k, t], w, start=(k == 0), stop=False)
                    last = pe.matmul(to, h_lo[r.p][:, k, t], w, start=False, stop=(not general and k == KH - 1))
                    if general:
                        w_lo = wring[:, blocks[k // 4] % ring.slots, (k % 4) * D:(k % 4 + 1) * D]
                        last = pe.matmul(to, h_hi[r.p][:, k, t], w_lo, start=False, stop=(k == KH - 1))
                    return last

                for n in range(NB):
                    pe.wait_ge(f_lo, r.at(LO, LO - 3 + n))
                    for k in range(KH - 1):
                        if n == 0 and k > 4:
                            pe.wait_ge(f_lo, r.at(LO, LO - KH + k + 1))
                        part(n, k)
                for n in range(NB):
                    part(n, KH - 1).then_inc(f_mm, 1)

            def a_turn(a):
                pe.wait_ge(a_norm, a.at(1, 1))
                for kc in range(KD):
                    for n in range(SB):
                        last = pe.transpose(ab[0][:, kc * ST + n * P:kc * ST + (n + 1) * P],
                                            a_hat[:, n, kc * P:(kc + 1) * P], ident[:, :])
                last.then_inc(a_turned, 1)

            def a_project(a):
                pe.wait_ge(a_xT, a.at(1, 1))
                for w in range(4):
                    if w == 1:
                        after(pe, a_otmp, a.at(1, 0))
                    bank = ab[(1, 2, 3, 0)[w]]
                    for e in range(2):
                        for k in range(KD):
                            last = pe.matmul(bank[:, e * ST:(e + 1) * ST],
                                             wproj[:, k, w * D + e * P:w * D + (e + 1) * P], aT[:, k, :],
                                             start=(k == 0), stop=(k == KD - 1))
                    last.then_inc(a_proj, 1)

            def a_sum_heads(a, k):
                j = valid[a.c][k]
                g, jl = j // 8, j % 8
                v = valid[a.c]
                final = k + 1 == len(v) or v[k + 1] // 8 != g
                lo = 0 if jl == 0 else max(0, UNIQUE[j] - ST * a.c)
                rows_ = P if g < 2 else len(GROUPS[g]) * HEADS
                bank = ab[1 + g // 2]
                o = (7 - jl) * HEADS
                pe.wait_ge(a_fold, per_offset.at(a, k + 1))
                pe.matmul(bank[0:rows_, (g % 2) * ST + lo:(g % 2 + 1) * ST], sel_in[:, o:o + rows_],
                          fold[:, k % 4, lo:ST], start=(jl == 0), stop=final).then_inc(a_scored, 1)

            def a_sturn(a):
                gs = groups_of[a.c]
                pe.wait_ge(a_scopied, per_half.at(a, 2 if len(gs) > 2 else 1))
                for n in range(SB):
                    bank = ab[3] if n == 0 else ab[0]
                    for g in gs:
                        rows_ = P if g < 2 else 64
                        last = pe.transpose(bank[:, g * P:g * P + rows_], sT[0:rows_, g, n * P:(n + 1) * P],
                                            ident[0:rows_, 0:rows_])
                    last.then_inc(a_sturned, 1)

            def a_pturn(a):
                gs = groups_of[a.c]
                pe.wait_ge(a_probs, a.at(1, 1))
                for n in range(SB):
                    for g in range(2):
                        last = pe.transpose(ab[1][:, g * ST + n * P:g * ST + (n + 1) * P],
                                            S[:, n, g * P:(g + 1) * P], ident[:, :])
                last.then_inc(a_pturned, 1)
                if len(gs) > 2:
                    for n in range(SB):
                        last = pe.transpose(ab[2][0:64, n * P:(n + 1) * P], S[:, n, 2 * P:2 * P + 64], ident[:, :])
                    last.then_inc(a_pturned, 1)

            def a_spread(a, pair):
                v = valid[a.c]
                bank = ab[(3, 0, 1)[pair % 3]]
                if pair == 0:
                    pe.wait_ge(a_plo, per_half.at(a, 2 if len(groups_of[a.c]) > 2 else 1))
                if pair >= 3:
                    pe.wait_ge(a_pv, per_later_offset.at(a, 2 * (pair - 3) + 1))
                for k in range(2 * pair, min(2 * pair + 2, len(v))):
                    g, jl = v[k] // 8, v[k] % 8
                    rows_ = P if g < 2 else 64
                    to = bank[:, (k % 2) * ST:(k % 2 + 1) * ST]
                    pe.matmul(to, sel_out[0:rows_, jl, :], p_hi[0:rows_, g, :], start=True, stop=False)
                    last = pe.matmul(to, sel_out[0:rows_, jl, :], p_lo[0:rows_, g, :], start=False, stop=True)
                last.then_inc(a_spread_done, 1)

            

            def a_wout(a):
                pe.wait_ge(a_z, a.at(1, 1))
                for n in range(SB):
                    for e in range(2):
                        last = pe.matmul(ab[2][:, n * D:(n + 1) * D], acc[:, e, n * P:(n + 1) * P], wo[:, e, :],
                                         start=(e == 0), stop=(e == 1))
                last.then_inc(a_wo, 1)

            def run(general):
                ring = Ring(general)
                schedule(pe, {
                    "f_turn": f_turn,
                    "f_in": lambda r, m: run_in(r, m, ring, general),
                    "f_hidden": lambda r, layer, m: run_hidden(r, layer, m, ring, general),
                    "f_out": lambda r: run_out(r, ring, general),
                    "a_turn": a_turn, "a_project": a_project, "a_sum_heads": a_sum_heads, "a_sturn": a_sturn,
                    "a_pturn": a_pturn, "a_spread": a_spread, "a_wout": a_wout,
                }, at="start")

            with pe.If(has_lo != 0):
                run(True)
            with pe.Else():
                run(False)


def _lay_out(inputs):
    import numpy as np
    g = {k: np.asarray(v) for k, v in inputs.items()}
    P, heads, dh, d, hid = 128, 16, 16, 256, 1024
    kh, kd = hid // P, d // P
    blocks = []
    for n in ("h1", "h2"):
        w = g[f"L0_ffn_{n}_w"].reshape(kh, P, kh, P)
        blocks.append(w.transpose(0, 3, 2, 1).reshape(kh, P, kh * P))
    w12 = np.stack([g["L0_ffn_w1_w"], g["L0_ffn_w2_w"]]).reshape(2, kh // 2, 2, P, kd, P)
    blocks.append(w12.transpose(1, 5, 2, 0, 4, 3).reshape(kh // 2, P, 8 * P))
    w3 = g["L0_ffn_w3_w"].reshape(d, 2, 4, P)
    blocks.append(w3.transpose(1, 3, 2, 0).reshape(2, P, 4 * d))
    ffn_w = np.concatenate(blocks)

    def split_heads(a, axis):
        s = a.shape
        a = a.reshape(s[:axis] + (-1, heads, 2, dh // 2) + s[axis + 1:])
        return np.moveaxis(a, axis + 2, axis + 1).reshape(s)

    proj = np.concatenate([split_heads(g["L0_attn_Wqkv"], 1), split_heads(g["L0_attn_Wgate"], 1)], axis=1)
    proj_w = proj.reshape(kd, P, 4 * d).transpose(1, 0, 2)
    out_w = split_heads(g["L0_attn_Wout"], 0).reshape(2, P, d).transpose(1, 0, 2)
    scales = [g[f"L0_ffn_{n}_s"].reshape(kh, P) for n in ("w1", "w2", "h1", "h2")]
    cols = np.concatenate(scales + [split_heads(g["L0_attn_bqkv"], 0).reshape(6, P),
                                    split_heads(g["L0_attn_bgate"], 0).reshape(2, P)]).T
    first = [OFFSETS.index(o) for o in UNIQUE]
    second = [len(OFFSETS) - 1 - OFFSETS[::-1].index(o) for o in TWICE]
    rows = np.concatenate([g["L0_ffn_w3_s"], g["L0_attn_bout"], g["L0_attn_pos_bias"][first + second].reshape(-1)])
    masks = np.zeros((P, P + 15 * heads + 8 * P), np.float32)
    p = np.arange(P)
    masks[p, p] = 1.0
    masks[p, P + 7 * heads + p // 8] = 1.0
    for j in range(8):
        f = np.arange(P)
        masks[heads * j + f // 8, P + 15 * heads + j * P + f] = 1.0
    return {"x": g["L0_attn_x"], "ffn_w": ffn_w, "proj_w": proj_w, "out_w": out_w, "cols": cols,
            "rows": rows, "masks": masks}


def kernel(**inputs):
    import numpy as np
    import concourse.bacc as bacc
    from concourse.bass_utils import run_bass_kernel_spmd

    nc = bacc.Bacc("TRN2", target_bir_lowering=False, num_devices=1)
    arrays, args = {}, []
    for name, a in _lay_out(inputs).items():
        a = np.ascontiguousarray(a)
        arrays[f"in_{name}"] = a
        args.append(nc.dram_tensor(f"in_{name}", a.shape, mybir.dt.from_np(a.dtype), kind="ExternalInput").ap())
    shape = arrays["in_x"].shape
    args.append(nc.dram_tensor("out_x", shape, mybir.dt.float32, kind="ExternalOutput").ap())
    macaron_kernel(nc, *args)
    r = run_bass_kernel_spmd(nc, [arrays], core_ids=[0])
    return r.results[0]["out_x"]
```

```python
import concourse.bass as bass
from concourse import mybir
from contextlib import ExitStack

OFFSETS = [0, 1, 2, 3, 4, 6, 8, 12, 16, 24, 32, 48, 64, 96, 128, 192, 64, 96, 128, 192, 256, 384, 512, 768]
UNIQUE = sorted(set(OFFSETS))
TWICE = [o for o in UNIQUE if OFFSETS.count(o) == 2]
EPS = 1e-5


class Counts:

    def __init__(self, per_subtile):
        self.total = sum(per_subtile)
        self.before = [sum(per_subtile[:c]) for c in range(len(per_subtile))]

    def at(self, sub, k):
        return sub.batch * self.total + (self.before[sub.c] + k)


class Ffn:

    def __init__(self, half_number, parity, tile, second, last=False):
        self.h, self.p, self.tile, self.second, self.last = half_number, parity, tile, second, last

    def at(self, per_run, k):
        return self.h * (2 * per_run) + (self.p * per_run + k)


class Sub:

    def __init__(self, batch, c, per_batch):
        self.batch, self.c, self.per_batch = batch, c, per_batch

    def at(self, per_sub, k):
        return self.batch * (self.per_batch * per_sub) + (self.c * per_sub + k)


def after(eng, sem, value):
    if not (isinstance(value, int) and value <= 0):
        eng.wait_ge(sem, value)


def macaron_kernel(nc, x, ffn_w, proj_w, out_w, cols, rows, masks, out):
    fp32, fp32r = mybir.dt.float32, mybir.dt.float32r
    ALU, ACT, AX = mybir.AluOpType, mybir.ActivationFunctionType, mybir.AxisListType

    P = 128
    B, N, D = x.shape
    HEADS = 16
    DH = D // HEADS
    KD = D // P
    HID = 1024
    KH = HID // P
    TT = 512
    NB = TT // P
    TILES = B * N // TT
    TPB = N // TT
    ST = 256
    SB = ST // P
    SUBS = N // ST
    NU, NE = len(UNIQUE), len(OFFSETS)
    ROWS = HEADS * NU
    GROUPS = [list(range(g, min(g + 8, NU))) for g in range(0, NU, 8)]
    FOLD_ROWS = P // HEADS
    SCALE = DH ** -0.5
    FIRST_TWICE = UNIQUE.index(TWICE[0]) * HEADS
    WBLK = 1024
    H_BLOCKS, IN_BLOCKS, OUT_BLOCKS = 2 * KH, 4, 2
    BLOCKS = H_BLOCKS + IN_BLOCKS + OUT_BLOCKS

    valid = [[j for j, o in enumerate(UNIQUE) if o < ST * (c + 1)] for c in range(SUBS)]
    groups_of = [[g for g in range(3) if GROUPS[g][0] in valid[c]] for c in range(SUBS)]
    per_offset = Counts([len(v) for v in valid])
    per_later_offset = Counts([len(v) - 1 for v in valid])
    per_pair = Counts([(len(v) + 1) // 2 for v in valid])
    per_half = Counts([1 if len(g) == 2 else 2 for g in groups_of])

    OB = NB // 2
    MM = 2 * KH + KH + KH + OB
    TURN = 2 * KH + KH
    BANKS = MM + 2
    LO = 3 * KH
    RING = 6

    x_rows = x.rearrange("b (t n p) d -> (b t) p n d", n=NB, p=P)
    x1 = nc.dram_tensor("x_after_ffn1", (TILES, P, NB, D), fp32)
    x2 = nc.dram_tensor("x_after_attention", (TILES, P, NB, D), fp32)
    out_rows = out.rearrange("b (t n p) d -> (b t) p n d", n=NB, p=P)
    hi_dram = nc.dram_tensor("weights_hi", (H_BLOCKS, P, WBLK), fp32)
    lo_dram = nc.dram_tensor("weights_lo", (BLOCKS, P, WBLK), fp32)

    ctx = ExitStack()
    with ctx:
        def sb(name, shape, dt=fp32):
            return ctx.enter_context(nc.sbuf_tensor(name, shape, dt))

        def sem(name):
            return ctx.enter_context(nc.semaphore(name))

        w_in = sb("w_in", [P, IN_BLOCKS, WBLK], fp32r)
        w_out3 = sb("w_out3", [P, OUT_BLOCKS, WBLK], fp32r)
        wring = sb("wring", [P, 4, WBLK], fp32r)
        wproj = sb("wproj", [P, KD, 4 * D])
        wo = sb("wo", [P, KD, D])
        colv = sb("colv", [P, 40])
        rowv = sb("rowv", [P, 2 * D + NE * HEADS])
        ident = sb("ident", [P, P])
        differ = sb("differ", [P, BLOCKS])
        differ_sum = sb("differ_sum", [P, 1])
        ones = sb("ones", [P, 1])
        flag = sb("flag", [1, 1], mybir.dt.int32)
        sel_in = sb("sel_in", [P, 15 * HEADS])
        sel_out = sb("sel_out", [P, 8, P], fp32r)
        half_neg = sb("half_neg", [P, NB])
        xf = sb("xf", [P, 2, NB, D])
        f_hat = sb("f_hat", [P, 2, D])
        fT_hi = sb("fT_hi", [P, KD, TT], fp32r)
        fT_lo = sb("fT_lo", [P, KD, TT], fp32r)
        h_hi = [sb(f"h_hi{i}", [P, KH, TT], fp32r) for i in range(2)]
        h_lo = [sb(f"h_lo{i}", [P, KH, TT], fp32r) for i in range(2)]
        f_gated = sb("f_gated", [P, 3, TT])
        f_st = sb("f_st", [P, NB, 6])
        f_mo = sb("f_mo", [P, 5, NB])
        f_mean = sb("f_mean", [P, NB])
        f_var = sb("f_var", [P, NB])
        f_rs = sb("f_rs", [P, NB])
        xa = sb("xa", [P, 2, SB, D])
        aT = sb("aT", [P, KD, ST])
        q = sb("q", [P, 2, ST])
        keys = sb("keys", [P, 2, N])
        vals = sb("vals", [P, 2, N])
        gate = sb("gate", [P, 2, ST])
        prod = sb("prod", [P, RING, 2, ST])
        fold = sb("fold", [P, RING, ST])
        sT = sb("sT", [P, 3, ST])
        a_hat = sT[:, 0:2, :]
        S = sb("S", [P, SB, NE * HEADS])
        p_hi = sb("p_hi", [P, 3, ST], fp32r)
        p_lo = sb("p_lo", [P, 3, ST], fp32r)
        acc = sb("acc", [P, 2, ST])
        a_st = sb("a_st", [P, SB, 6])
        a_mo = sb("a_mo", [P, 5, SB])
        a_mean = sb("a_mean", [P, SB])
        a_var = sb("a_var", [P, SB])
        a_rs = sb("a_rs", [P, SB])
        mx = sb("mx", [P, SB, HEADS])
        sm = sb("sm", [P, SB, HEADS])

        fb = [ctx.enter_context(nc.psum_tensor(f"f_bank{i}", [P, 512], fp32)) for i in range(4)]
        ab = [ctx.enter_context(nc.psum_tensor(f"a_bank{i}", [P, 512], fp32)) for i in range(4)]

        def w12(m, w, k):
            o = ((m % 2) * 4 + w * 2 + k) * P
            return w_in[:, m // 2, o:o + P]

        def scale_col(layer, m):
            return colv[:, layer * KH + m:layer * KH + m + 1]

        qkv_bias = [[colv[:, 32 + 2 * w + e:33 + 2 * w + e] for e in range(2)] for w in range(3)]
        gate_bias = [colv[:, 38 + e:39 + e] for e in range(2)]
        s3 = rowv[:, 0:D]
        bout = rowv[:, D:2 * D]
        pos = rowv[:, 2 * D:]

        s_const = sem("s_const")
        s_mask = sem("s_mask")
        s_stage = [sem(f"s_stage{i}") for i in range(4)]
        s_ident = sem("s_ident")
        s_hi = sem("s_hi")
        s_compared = sem("s_compared")
        s_stored = [sem(f"s_stored{i}") for i in range(4)]
        s_counted, s_summed, s_flag = sem("s_counted"), sem("s_summed"), sem("s_flag")
        g_stage = [sem(f"g_stage{i}") for i in range(2)]
        g_hi, g_lo = sem("g_hi"), sem("g_lo")
        g_stored = [sem(f"g_stored{i}") for i in range(2)]
        s_sel = sem("s_sel")
        s_scaled = sem("s_scaled")
        s_neg = sem("s_neg")
        s_stores_seen = sem("s_stores_seen")
        s_ring = [sem(f"s_ring{i}") for i in range(4)]
        f_loaded = [sem(f"f_loaded{i}") for i in range(2)]
        f_stored = [sem(f"f_stored{i}") for i in range(2)]
        f_stats, f_summed, f_squared = sem("f_stats"), sem("f_summed"), sem("f_squared")
        f_vareps, f_rstd = sem("f_vareps"), sem("f_rstd")
        f_norm, f_turned, f_thi, f_tlo = sem("f_norm"), sem("f_turned"), sem("f_thi"), sem("f_tlo")
        f_mm, f_silu, f_prod, f_phi = sem("f_mm"), sem("f_silu"), sem("f_prod"), sem("f_phi")
        f_gelu, f_lo, f_outs, f_x = sem("f_gelu"), sem("f_lo"), sem("f_outs"), sem("f_x")
        a_loaded = [sem(f"a_loaded{i}") for i in range(2)]
        a_stored = [sem(f"a_stored{i}") for i in range(2)]
        a_stats, a_summed, a_squared = sem("a_stats"), sem("a_summed"), sem("a_squared")
        a_vareps, a_rstd = sem("a_vareps"), sem("a_rstd")
        a_norm, a_turned, a_xT = sem("a_norm"), sem("a_turned"), sem("a_xT")
        a_proj, a_qkv, a_gexp = sem("a_proj"), sem("a_qkv"), sem("a_gexp")
        a_gone, a_gate = sem("a_gone"), sem("a_gate")
        a_qk, a_fold, a_scored = sem("a_qk"), sem("a_fold"), sem("a_scored")
        a_scopied, a_sturned, a_biased = sem("a_scopied"), sem("a_sturned"), sem("a_biased")
        a_max, a_less, a_exp, a_sum = sem("a_max"), sem("a_less"), sem("a_exp"), sem("a_sum")
        a_recip, a_probs, a_pturned = sem("a_recip"), sem("a_probs"), sem("a_pturned")
        a_phi, a_plo, a_spread_done = sem("a_phi"), sem("a_plo"), sem("a_spread_done")
        a_pv, a_acc, a_z = sem("a_pv"), sem("a_acc"), sem("a_z")
        a_wo, a_otmp, a_x = sem("a_wo"), sem("a_otmp"), sem("a_x")

        staged = [vals[:, 0, :], vals[:, 1, :]] + [
            prod[:, 2 * i:2 * i + 2, :, :].rearrange("p a e n -> p (a e n)") for i in range(2)]
        sel_staged = keys[:, 0, :]

        def h_slot(buffer, s):
            return buffer[:, 2 * s:2 * s + 2, :].rearrange("p a n -> p (a n)")

        block = ctx.enter_context(nc.Block())

        FIRST = Ffn(0, 0, 0, False)
        LAST_FIRST = Ffn(TILES - 3, 1, TILES - 1, False)
        FFN_TIME = KH * 1.7 + 2 * KH * 3.4 + 6.8

        def schedule(eng, do, at="end", ahead=0, late=(0.0, 0.0, 0.0)):

            def ffn_steps(r, following, now):
                steps = []

                def add(time, name, *args, late=0.0):
                    nonlocal now
                    place = now - ahead if at == "start" else now + time + late
                    steps.append((place, name, args))
                    now += time

                for m in range(KH + 1):
                    add(1.7 if m < KH else 0.0, "f_in", r, m, late=late[0] if m < KH - 1 else 0.0)
                inside = {(0, 3): ("f_load", ()), (0, 5): ("f_norm", ()),
                          (1, 0): ("f_turn", (0, r)), (1, 1): ("f_turn", (1, r))}
                for layer in range(2):
                    for m in range(KH):
                        add(3.4, "f_hidden", r, layer, m, late=late[1] if m < KH - 1 else 0.0)
                        if following is not None and (layer, m) in inside:
                            name, args = inside[layer, m]
                            steps.append((now, name, (following, *args)))
                add(6.8, "f_out", r, late=late[2])
                steps.append((now + (5 if ahead else 0), "f_store", (r,)))
                return steps

            def attention_steps(a, tile, u, start, span):
                v = valid[a.c]
                steps = [(-8, "a_load", (tile, u)), (-4, "a_norm", (a,)), (2, "a_turn", (a,)), (4, "a_project", (a,)),
                         (27, "a_gate", (a,))]
                for k in range(len(v)):
                    steps.append((9 + 0.9 * k, "a_score", (a, k)))
                    steps.append((13.5 + 0.9 * k, "a_sum_heads", (a, k)))
                now = 13.5 + 0.9 * len(v)
                steps += [(now + 1, "a_scopy", (a,)), (now + 2, "a_sturn", (a,)), (now + 4, "a_softmax", (a,)),
                          (now + 12, "a_pturn", (a,)), (now + 13, "a_pcut", (a,))]
                now += 15
                for k in range(len(v)):
                    if k % 2 == 0:
                        steps.append((now + 1.3 * k, "a_spread", (a, k // 2)))
                    steps.append((now + 4.5 + 1.3 * k, "a_weigh", (a, k)))
                now += 1.3 * len(v) + 6
                steps += [(now, "a_gated", (a,)), (now + 7, "a_wout", (a,)), (now + 8, "a_residual", (a, u)),
                          (now + 10, "a_store", (a, tile, u))]
                return [(start + t * span / (now + 10), name, args) for t, name, args in steps]

            def together(runs, tiles):
                steps = []
                for i, (r, following) in enumerate(zip(runs, runs[1:])):
                    steps += ffn_steps(r, following, i * FFN_TIME)
                for batch, c, tile, start, time in tiles:
                    for u in range(2):
                        steps += attention_steps(Sub(batch, c + u, SUBS), tile, u, start + time / 2 * u, time / 2)
                for _, name, args in sorted(steps, key=lambda s: s[0]):
                    if name in do:
                        do[name](*args)

            def ffn1(tile):
                return Ffn(tile - 1, 0, tile, False)

            def ffn2(tile):
                return Ffn(tile + 1, 1, tile, True)

            together([FIRST, Ffn(0, 1, 1, False), ffn1(2)], [(0, 0, 0, FFN_TIME + 9, FFN_TIME)])

            if "head_stored" in do:
                do["head_stored"]()

            with eng.Fori(1, TILES // 2 - 1) as k:
                for odd in range(2):
                    i = k * 2 + odd
                    together([ffn1(i), ffn2(i - 2), ffn1(i + 1)],
                             [(k - 1 + odd, 2 - 2 * odd, i - 1, 1, 2 * FFN_TIME - 3)])

            n = TILES
            tail = [ffn1(n - 2), LAST_FIRST, Ffn(n - 2, 0, n - 4, True), ffn2(n - 3), Ffn(n - 1, 0, n - 2, True),
                    Ffn(n - 1, 1, n - 1, True, last=True), None]
            together(tail, [(B - 2, SUBS - 2, n - 3, 1, 107), (B - 1, 0, n - 2, 109, 107),
                            (B - 1, SUBS - 2, n - 1, 217, 107)])

        class Ring:

            def __init__(self, general):
                blocks = []
                for j in range(IN_BLOCKS if general else 0):
                    blocks.append(("lo", H_BLOCKS + j, ("f_in", 2 * j), 4 * (j + 1)))
                for layer in range(2):
                    for m in range(KH):
                        for source in ("hi", "lo")[:2 if general else 1]:
                            n = 2 * KH + layer * KH + m + 1
                            blocks.append((source, layer * KH + m, ("f_hidden", layer, m), n))
                for j in range(OUT_BLOCKS if general else 0):
                    blocks.append(("lo", H_BLOCKS + IN_BLOCKS + j, ("f_out",), MM))
                self.blocks, self.slots = blocks, 2 if general else 4
                assert len(blocks) % self.slots == 0

            def of_step(self, *step):
                return [i for i, b in enumerate(self.blocks) if b[2] == step]

            def filled(self, r, i):
                return r.at(16 * (len(self.blocks) // self.slots), 16 * (i // self.slots + 1))

            def freed(self, r, i):
                return r.at(MM, self.blocks[i - self.slots][3] if i >= self.slots else 0)

        def f_bank(r, n):
            return fb[(r.p * BANKS + n) % 4]

        def turn_bank(r, bp):
            return fb[((1 - r.p) * BANKS + TURN + bp) % 4]

        def out_bank(r, n):
            return f_bank(r, TURN + 2 + KH + n)

        def hidden_use(layer, m):
            return 2 * KH + m if layer == 0 else TURN + 2 + m

        @block.sync
        def _(sp):
            def f_load(r):
                src = x2[r.tile, :, :, :] if r.second else x_rows[r.tile, :, :, :]
                sp.dma_start(xf[:, r.p, :, :], src).then_inc(f_loaded[r.p], 16)

            def stage(i, s):
                sp.dma_start(staged[s], ffn_w[i, :, :]).then_inc(s_stage[s], 16)

            f_load(FIRST)
            stage(0, 0)
            stage(1, 1)
            sp.dma_start(sel_staged, masks[:, P + 15 * HEADS:]).then_inc(s_mask, 16)
            sp.dma_start(ident[:, :], masks[:, 0:P]).then_inc(s_ident, 16)
            stage(2, 2)
            stage(3, 3)
            with sp.Fori(0, H_BLOCKS // 4) as it:
                for s in range(4):
                    sp.wait_ge(s_compared, it * 4 + (s + 1))
                    sp.dma_start(hi_dram[it * 4 + s, :, :], h_slot(h_hi[0], s).bitcast(fp32)).then_inc(s_stored[s], 16)
                    stage(it * 4 + s + 4, s)
            for i in range(H_BLOCKS + 4, BLOCKS):
                sp.wait_ge(s_compared, i - 3)
                stage(i, i % 4)
            sp.dma_start(colv[:, :], cols).then_inc(s_const, 16)
            sp.dma_start(rowv[:, :], rows.partition_broadcast(P)).then_inc(s_const, 16)
            sp.dma_start(sel_in[:, :], masks[:, P:P + 15 * HEADS]).then_inc(s_const, 16)
            sp.dma_start(wproj[:, :, :], proj_w).then_inc(s_const, 16)
            sp.dma_start(wo[:, :, :], out_w).then_inc(s_const, 16)
            for s in range(4):
                sp.wait_ge(s_stored[s], 16 * (H_BLOCKS // 4))
            sp.wait_ge(s_flag, 1)
            has_lo = sp.value_load(flag[0:1, 0:1])

            def lo_parts():
                def load(i, slot):
                    sp.dma_start(staged[slot], ffn_w[i, :, :]).then_inc(g_stage[slot], 16)

                def store(i, slot):
                    sp.dma_start(lo_dram[i, :, :], h_slot(h_lo[0], slot).bitcast(fp32)).then_inc(g_stored[slot], 16)

                load(0, 0)
                load(1, 1)
                with sp.Fori(0, BLOCKS // 2 - 1) as it:
                    for slot in range(2):
                        sp.wait_ge(g_lo, it * 2 + (slot + 1))
                        store(it * 2 + slot, slot)
                        load(it * 2 + slot + 2, slot)
                for slot in range(2):
                    sp.wait_ge(g_lo, BLOCKS - 1 + slot)
                    store(BLOCKS - 2 + slot, slot)
                for slot in range(2):
                    sp.wait_ge(g_stored[slot], 16 * (BLOCKS // 2))

            def wait_alone(semaphore, value):
                after(sp, semaphore, value)
                sp.sem_inc(s_stores_seen, 1)

            def f_load_(r):
                wait_alone(f_stored[r.p], r.h * 16)
                if r.second:
                    for u in range(2):
                        wait_alone(a_stored[u], r.tile * 16 + 16)
                f_load(r)

            def f_store(r):
                sp.wait_ge(f_x, r.at(OB, OB))
                dst = out_rows if r.second else x1
                sp.dma_start(dst[r.tile, :, :, :], xf[:, r.p, :, :]).then_inc(f_stored[r.p], 16)

            def a_load(tile, u):
                wait_alone(a_stored[u], tile * 16)
                if isinstance(tile, int) and tile < 2:
                    wait_alone(f_stored[tile], 16)
                elif isinstance(tile, int) and tile == LAST_FIRST.tile:
                    wait_alone(f_stored[1], LAST_FIRST.h * 16 + 16)
                else:
                    wait_alone(f_stored[0], tile * 16)
                sp.dma_start(xa[:, u, :, :], x1[tile, :, u * SB:(u + 1) * SB, :]).then_inc(a_loaded[u], 16)

            def a_store(a, tile, u):
                sp.wait_ge(a_x, a.at(1, 1))
                sp.dma_start(x2[tile, :, u * SB:(u + 1) * SB, :], xa[:, u, :, :]).then_inc(a_stored[u], 16)

            def run(general):
                ring = Ring(general)
                sources = {"hi": hi_dram, "lo": lo_dram}

                def fill(r, *step):
                    for i in ring.of_step(*step):
                        source, blk, _, _ = ring.blocks[i]
                        after(sp, f_mm, ring.freed(r, i))
                        sp.dma_start(wring[:, i % ring.slots, :].bitcast(fp32),
                                     sources[source][blk, :, :])\
                            .then_inc(s_ring[i % ring.slots], 16)

                schedule(sp, {
                    "head_stored": lambda: wait_alone(f_stored[1], 16),
                    "f_load": f_load_, "f_store": f_store, "a_load": a_load, "a_store": a_store,
                    "f_in": lambda r, m: fill(r, "f_in", m),
                    "f_hidden": lambda r, layer, m: fill(r, "f_hidden", layer, m),
                    "f_out": lambda r: fill(r, "f_out"),
                }, at="start", ahead=3 if general else 7)

            with sp.If(has_lo != 0):
                lo_parts()
                run(True)
            with sp.Else():
                run(False)
            for p in range(2):
                sp.wait_ge(f_stored[p], 16 * TILES)
                sp.wait_ge(a_stored[p], 16 * TILES)

        @block.gpsimd
        def _(pool):
            pool.memset(half_neg[:, :], -0.5).then_inc(s_neg, 1)
            pool.wait_ge(s_neg, 1)

            def f_norm_(r):
                pool.wait_ge(f_vareps, r.at(1, 1))
                pool.tensor_tensor(f_rs[:, :], f_var[:, :], half_neg[:, :], ALU.pow).then_inc(f_rstd, 1)

            def a_norm_(a):
                pool.wait_ge(a_vareps, a.at(1, 1))
                pool.tensor_tensor(a_rs[:, :], a_var[:, :], half_neg[:, 0:SB], ALU.pow).then_inc(a_rstd, 1)

            def a_score(a, k):
                lo = max(0, UNIQUE[valid[a.c][k]] - ST * a.c)
                pool.wait_ge(a_qk, per_offset.at(a, k + 1))
                if k >= RING:
                    pool.wait_ge(a_scored, per_offset.at(a, k - RING + 1))
                else:
                    after(pool, a_scored, per_offset.at(a, 0))
                last = pool.tensor_tensor(fold[:, k % RING, lo:ST], prod[:, k % RING, 0, lo:ST],
                                          prod[:, k % RING, 1, lo:ST], ALU.add)
                if lo and valid[a.c][k] % 8 == 0:
                    last = pool.memset(fold[:, k % RING, 0:lo], 0.0)
                last.then_inc(a_fold, 1)

            def a_weigh(a, k):
                if k == 0:
                    return
                lo = max(0, UNIQUE[valid[a.c][k]] - ST * a.c)
                pool.wait_ge(a_pv, per_later_offset.at(a, k))
                pool.wait_ge(a_acc, per_offset.at(a, k))
                pool.tensor_tensor(acc[:, :, lo:ST], acc[:, :, lo:ST], prod[:, k % RING, :, lo:ST], ALU.add)\
                    .then_inc(a_acc, 1)

            f_norm_(FIRST)
            schedule(pool, {"f_norm": f_norm_, "a_norm": a_norm_, "a_score": a_score, "a_weigh": a_weigh})

        @block.scalar
        def _(act):
            def f_turn(r, bp, before):
                act.wait_ge(f_turned, r.at(2, bp + 1))
                act.activation(fT_hi[:, :, bp * ST:(bp + 1) * ST],
                               turn_bank(r, bp)[:, :].rearrange("p (k n) -> p k n", k=KD), ACT.Copy)\
                    .then_inc(f_thi, 1)

            act.wait_ge(s_mask, 16)
            act.activation(sel_out[:, :, :].rearrange("p j f -> p (j f)"), sel_staged, ACT.Copy).then_inc(s_sel, 1)

            def cut_hi(s, stage_value, dst):
                act.wait_ge(s_stage[s], stage_value)
                act.activation(dst, staged[s], ACT.Copy).then_inc(s_hi, 1)

            for s in range(4):
                cut_hi(s, 16, h_slot(h_hi[0], s))
            with act.Fori(1, H_BLOCKS // 4) as it:
                for s in range(4):
                    act.wait_ge(s_stored[s], it * 16)
                    cut_hi(s, it * 16 + 16, h_slot(h_hi[0], s))
            f_turn(FIRST, 0, None)
            f_turn(FIRST, 1, None)
            for i in range(H_BLOCKS, BLOCKS):
                j = i - H_BLOCKS
                dst = w_in[:, j, :] if j < IN_BLOCKS else w_out3[:, j - IN_BLOCKS, :]
                cut_hi(i % 4, 16 * (i // 4 + 1), dst)
            act.wait_ge(s_scaled, 3)

            def f_in(r, m):
                if m < KH:
                    bank = f_bank(r, 2 * m)
                    act.wait_ge(f_mm, r.at(MM, 2 * m + 1))
                    if m >= 3:
                        act.wait_ge(f_lo, r.at(LO, m - 2))
                    act.activation(f_gated[:, m % 3, :], bank[:, :], ACT.Silu, scale=scale_col(0, m)).then_inc(f_silu, 1)
                if m > 0:
                    act.wait_ge(f_prod, r.at(KH, m))
                    act.activation(h_hi[r.p][:, m - 1, :], f_gated[:, (m - 1) % 3, :], ACT.Copy).then_inc(f_phi, 1)

            def f_hidden(r, layer, m):
                n = 2 * KH + layer * KH + m
                bank, dst = f_bank(r, hidden_use(layer, m)), h_hi[(r.p + 1 + layer) % 2]
                act.wait_ge(f_mm, r.at(MM, n + 1))
                act.activation(dst[:, m, :], bank[:, :], ACT.Gelu, scale=scale_col(2 + layer, m))
                act.activation(bank[:, :], bank[:, :], ACT.Gelu, scale=scale_col(2 + layer, m)).then_inc(f_gelu, 1)

            def a_turn(a):
                act.wait_ge(a_turned, a.at(1, 1))
                act.activation(aT[:, :, :].rearrange("p k n -> p (k n)"), ab[0][:, :], ACT.Copy).then_inc(a_xT, 1)

            def a_project(a):
                s0 = ST * a.c
                for w, dst in enumerate((q[:, :, :], keys[:, :, s0:s0 + ST], vals[:, :, s0:s0 + ST])):
                    act.wait_ge(a_proj, a.at(4, w + 1))
                    for e in range(2):
                        last = act.activation(dst[:, e, :], ab[1 + w][:, e * ST:(e + 1) * ST], ACT.Identity,
                                              bias=qkv_bias[w][e], scale=SCALE if w == 0 else 1.0)
                    last.then_inc(a_qkv, 1)
                act.wait_ge(a_proj, a.at(4, 4))
                for e in range(2):
                    last = act.activation(gate[:, e, :], ab[0][:, e * ST:(e + 1) * ST], ACT.Exp,
                                          bias=gate_bias[e], scale=-1.0)
                last.then_inc(a_gexp, 1)

            def a_scopy(a):
                v, gs = valid[a.c], groups_of[a.c]
                act.wait_ge(a_scored, per_offset.at(a, 16))
                act.activation(sT[:, 0:2, :].rearrange("p g n -> p (g n)"), ab[1][:, :], ACT.Copy).then_inc(a_scopied, 1)
                if len(gs) > 2:
                    act.wait_ge(a_scored, per_offset.at(a, len(v)))
                    act.activation(sT[0:64, 2, :], ab[2][0:64, 0:ST], ACT.Copy).then_inc(a_scopied, 1)

            def a_softmax(a):
                act.wait_ge(a_less, a.at(1, 1))
                act.activation(S[:, :, :], S[:, :, :], ACT.Exp).then_inc(a_exp, 1)

            def a_pcut(a):
                act.wait_ge(a_pturned, per_half.at(a, 1))
                act.activation(p_hi[:, 0:2, :].rearrange("p g n -> p (g n)"), ab[1][:, :], ACT.Copy).then_inc(a_phi, 1)
                if len(groups_of[a.c]) > 2:
                    act.wait_ge(a_pturned, per_half.at(a, 2))
                    act.activation(p_hi[0:64, 2, :], ab[2][0:64, 0:ST], ACT.Copy).then_inc(a_phi, 1)

            schedule(act, {"f_turn": f_turn, "f_in": f_in, "f_hidden": f_hidden, "a_turn": a_turn,
                           "a_project": a_project, "a_scopy": a_scopy, "a_softmax": a_softmax, "a_pcut": a_pcut})

        @block.vector
        def _(dve):
            def moments(run, st, mo, mean, var, stats, summed, squared, vareps):
                even, odd = (1, 2), (4, 5)
                dve.wait_ge(stats, run.at(1, 1))
                dve.tensor_tensor(mo[:, 0, :], st[:, :, even[0]], st[:, :, odd[0]], ALU.add)
                dve.tensor_tensor(mo[:, 1, :], st[:, :, even[0]], st[:, :, odd[0]], ALU.subtract)
                dve.tensor_tensor(mo[:, 2, :], st[:, :, even[1]], st[:, :, odd[1]], ALU.add).then_inc(summed, 1)
                dve.wait_ge(summed, run.at(1, 1))
                dve.tensor_scalar(mean[:, :], mo[:, 0, :], 0.5, None, ALU.mult)
                dve.tensor_tensor(mo[:, 3, :], mo[:, 1, :], mo[:, 1, :], ALU.mult)
                dve.tensor_scalar(mo[:, 4, :], mo[:, 2, :], 1.0 / D, EPS, ALU.mult, ALU.add).then_inc(squared, 1)
                dve.wait_ge(squared, run.at(1, 1))
                dve.scalar_tensor_tensor(var[:, :], mo[:, 3, :], 0.25, mo[:, 4, :], ALU.mult, ALU.add)\
                    .then_inc(vareps, 1)

            def f_norm_(r):
                dve.wait_ge(f_loaded[r.p], r.h * 16 + 16)
                for n in range(NB):
                    last = dve.bn_stats(f_st[:, n, :], xf[:, r.p, n, :])
                last.then_inc(f_stats, 1)
                moments(r, f_st, f_mo, f_mean, f_var, f_stats, f_summed, f_squared, f_vareps)
                dve.wait_ge(f_rstd, r.at(1, 1))
                f_scale(r, 0)

            def f_scale(r, bp):
                for n in range(2):
                    i = 2 * bp + n
                    last = dve.tensor_scalar(f_hat[:, n, :], xf[:, r.p, i, :], f_mean[:, i:i + 1],
                                             f_rs[:, i:i + 1], ALU.subtract, ALU.mult)
                last.then_inc(f_norm, 1)

            def f_turn(r, bp, before):
                if bp == 0:
                    dve.wait_ge(f_turned, r.at(2, 1))
                    f_scale(r, 1)
                dve.wait_ge(f_thi, r.at(2, bp + 1))
                part = slice(bp * ST, (bp + 1) * ST)
                dve.tensor_tensor(fT_lo[:, :, part], turn_bank(r, bp)[:, :].rearrange("p (k n) -> p k n", k=KD),
                                  fT_hi[:, :, part].bitcast(fp32), ALU.subtract).then_inc(f_tlo, 1)

            def compare(i, s, hi_value, hi, count):
                dve.wait_ge(s_hi, hi_value)
                dve.scalar_tensor_tensor(h_slot(h_lo[0], s), staged[s], 1.0, hi.bitcast(fp32),
                                         ALU.mult, ALU.not_equal, accum_out=count).then_inc(s_compared, 1)

            f_norm_(FIRST)
            with dve.Fori(0, H_BLOCKS // 4) as it:
                for s in range(4):
                    compare(it * 4 + s, s, it * 4 + (s + 1), h_slot(h_hi[0], s), differ[:, bass.ds(it * 4 + s, 1)])
            f_turn(FIRST, 0, None)
            f_turn(FIRST, 1, None)
            for i in range(H_BLOCKS, BLOCKS):
                j = i - H_BLOCKS
                hi = w_in[:, j, :] if j < IN_BLOCKS else w_out3[:, j - IN_BLOCKS, :]
                compare(i, i % 4, i + 1, hi, differ[:, i:i + 1])
            dve.wait_ge(s_compared, BLOCKS)
            dve.tensor_reduce(differ_sum[:, :], differ[:, :], AX.X, ALU.add)
            dve.memset(ones[:, :], 1.0).then_inc(s_summed, 1)
            dve.wait_ge(s_const, 16 * 5)
            dve.tensor_scalar(s3, s3, 0.5, None, ALU.mult).then_inc(s_scaled, 1)
            dve.tensor_scalar(colv[:, 32:34], colv[:, 32:34], SCALE, None, ALU.mult).then_inc(s_scaled, 1)
            dve.tensor_scalar(colv[:, 38:40], colv[:, 38:40], -1.0, None, ALU.mult).then_inc(s_scaled, 1)
            dve.wait_ge(s_scaled, 3)
            dve.wait_ge(s_counted, 1)
            dve.tensor_scalar(flag[:, :], ab[0][0:1, 0:1], 1.0, None, ALU.min).then_inc(s_flag, 1)
            dve.wait_ge(s_flag, 1)
            has_lo = dve.value_load(flag[0:1, 0:1])
            with dve.If(has_lo != 0):
                def cut_block(it, s, slot_used):
                    dve.wait_ge(g_stage[s], it * 16 + 16)
                    if slot_used:
                        dve.wait_ge(g_stored[s], it * 16)
                    dve.tensor_copy(h_slot(h_hi[0], s), staged[s]).then_inc(g_hi, 1)
                    dve.wait_ge(g_hi, it * 2 + (s + 1))
                    dve.tensor_tensor(h_slot(h_lo[0], s), staged[s], h_slot(h_hi[0], s).bitcast(fp32),
                                      ALU.subtract).then_inc(g_lo, 1)

                for s in range(2):
                    cut_block(0, s, False)
                with dve.Fori(1, BLOCKS // 2) as it:
                    for s in range(2):
                        cut_block(it, s, True)

            def f_in(r, m):
                if m < KH:
                    g, u = f_gated[:, m % 3, :], f_bank(r, 2 * m + 1)
                    dve.wait_ge(f_silu, r.at(KH, m + 1))
                    dve.wait_ge(f_mm, r.at(MM, 2 * m + 2))
                    dve.scalar_tensor_tensor(g, u[:, :], scale_col(1, m), g, ALU.mult, ALU.mult)\
                        .then_inc(f_prod, 1)
                if m > 0:
                    dve.wait_ge(f_phi, r.at(KH, m))
                    dve.tensor_tensor(h_lo[r.p][:, m - 1, :], f_gated[:, (m - 1) % 3, :],
                                      h_hi[r.p][:, m - 1, :].bitcast(fp32), ALU.subtract).then_inc(f_lo, 1)

            def f_hidden(r, layer, m):
                bank = f_bank(r, hidden_use(layer, m))
                i = (r.p + 1 + layer) % 2
                dve.wait_ge(f_gelu, r.at(2 * KH, layer * KH + m + 1))
                dve.tensor_tensor(h_lo[i][:, m, :], bank[:, :], h_hi[i][:, m, :].bitcast(fp32),
                                  ALU.subtract).then_inc(f_lo, 1)

            def f_out(r):
                for n in range(OB):
                    rows_ = xf[:, r.p, 2 * n:2 * n + 2, :]
                    dve.wait_ge(f_mm, r.at(MM, 4 * KH + n + 1))
                    bank = out_bank(r, n)[:, :].rearrange("p (n d) -> p n d", n=2)
                    dve.tensor_tensor(bank, bank, s3.unsqueeze(1).to_broadcast([P, 2, D]), ALU.mult)\
                        .then_inc(f_outs, 1)
                    dve.wait_ge(f_outs, r.at(OB, n + 1))
                    dve.tensor_tensor(rows_, rows_, bank, ALU.add).then_inc(f_x, 1)

            def a_norm_(a):
                u = a.c % 2
                dve.wait_ge(a_loaded[u], a.batch * (16 * TPB) + 16 * (a.c // 2 + 1))
                for n in range(SB):
                    last = dve.bn_stats(a_st[:, n, :], xa[:, u, n, :])
                last.then_inc(a_stats, 1)
                moments(a, a_st, a_mo, a_mean, a_var, a_stats, a_summed, a_squared, a_vareps)
                dve.wait_ge(a_rstd, a.at(1, 1))
                for n in range(SB):
                    last = dve.tensor_scalar(a_hat[:, n, :], xa[:, u, n, :], a_mean[:, n:n + 1],
                                             a_rs[:, n:n + 1], ALU.subtract, ALU.mult)
                last.then_inc(a_norm, 1)

            def a_gate_(a):
                dve.wait_ge(a_gexp, a.at(1, 1))
                dve.tensor_scalar(gate[:, :, :], gate[:, :, :], 1.0, None, ALU.add).then_inc(a_gone, 1)
                dve.wait_ge(a_gone, a.at(1, 1))
                for e in range(2):
                    last = dve.reciprocal(gate[:, e, :], gate[:, e, :])
                last.then_inc(a_gate, 1)

            def shifted(a, k):
                s0, o = ST * a.c, UNIQUE[valid[a.c][k]]
                lo = max(0, o - s0)
                return lo, slice(s0 - o + lo, s0 - o + ST)

            def a_score(a, k):
                lo, back = shifted(a, k)
                if k == 0:
                    dve.wait_ge(a_qkv, a.at(3, 3))
                if k >= RING:
                    dve.wait_ge(a_fold, per_offset.at(a, k - RING + 1))
                dve.tensor_tensor(prod[:, k % RING, :, lo:ST], q[:, :, lo:ST], keys[:, :, back], ALU.mult)\
                    .then_inc(a_qk, 1)

            def a_softmax(a):
                gs = groups_of[a.c]
                for n in range(SB):
                    bank = ab[3] if n == 0 else ab[0]
                    dve.wait_ge(a_sturned, a.at(SB, n + 1))
                    w = ROWS if len(gs) > 2 else 2 * P
                    dve.tensor_tensor(S[:, n, 0:w], bank[:, 0:w], pos[:, 0:w], ALU.add)
                    if w < ROWS:
                        dve.tensor_copy(S[:, n, w:ROWS], pos[:, w:ROWS])
                    dve.tensor_tensor(S[:, n, ROWS:], bank[:, FIRST_TWICE:FIRST_TWICE + len(TWICE) * HEADS],
                                      pos[:, ROWS:], ALU.add).then_inc(a_biased, 1)
                by_head = S[:, :, :].rearrange("p n (e h) -> p n h e", h=HEADS)
                by_entry = S[:, :, :].rearrange("p n (e h) -> p n e h", h=HEADS)
                dve.wait_ge(a_biased, a.at(SB, SB))
                dve.tensor_reduce(mx[:, :, :], by_head, AX.X, ALU.max).then_inc(a_max, 1)
                dve.wait_ge(a_max, a.at(1, 1))
                dve.tensor_tensor(by_entry, by_entry, mx[:, :, :].unsqueeze(2).to_broadcast([P, SB, NE, HEADS]),
                                  ALU.subtract).then_inc(a_less, 1)
                dve.wait_ge(a_exp, a.at(1, 1))
                dve.tensor_reduce(sm[:, :, :], by_head, AX.X, ALU.add).then_inc(a_sum, 1)
                dve.wait_ge(a_sum, a.at(1, 1))
                both = S[:, :, FIRST_TWICE:FIRST_TWICE + len(TWICE) * HEADS]
                dve.tensor_tensor(both, both, S[:, :, ROWS:], ALU.add)
                dve.reciprocal(sm[:, :, :], sm[:, :, :]).then_inc(a_recip, 1)
                dve.wait_ge(a_recip, a.at(1, 1))
                probs = S[:, :, 0:ROWS].rearrange("p n (e h) -> p n e h", h=HEADS)
                dve.tensor_tensor(probs, probs, sm[:, :, :].unsqueeze(2).to_broadcast([P, SB, NU, HEADS]),
                                  ALU.mult).then_inc(a_probs, 1)

            def a_pcut(a):
                gs = groups_of[a.c]
                dve.wait_ge(a_phi, per_half.at(a, 1))
                dve.tensor_tensor(p_lo[:, 0:2, :].rearrange("p g n -> p (g n)"), ab[1][:, :],
                                  p_hi[:, 0:2, :].rearrange("p g n -> p (g n)").bitcast(fp32), ALU.subtract)\
                    .then_inc(a_plo, 1)
                if len(gs) > 2:
                    dve.wait_ge(a_phi, per_half.at(a, 2))
                    dve.tensor_tensor(p_lo[0:64, 2, :], ab[2][0:64, 0:ST], p_hi[0:64, 2, :].bitcast(fp32),
                                      ALU.subtract).then_inc(a_plo, 1)

            def a_weigh(a, k):
                lo, back = shifted(a, k)
                bank = ab[(3, 0, 1)[k // 2 % 3]]
                if k % 2 == 0:
                    dve.wait_ge(a_spread_done, per_pair.at(a, k // 2 + 1))
                if k > RING:
                    dve.wait_ge(a_acc, per_offset.at(a, k - RING + 1))
                spread = bank[:, (k % 2) * ST + lo:(k % 2 + 1) * ST].unsqueeze(1).to_broadcast([P, 2, ST - lo])
                dst = acc[:, :, :] if k == 0 else prod[:, k % RING, :, lo:ST]
                dve.tensor_tensor(dst, vals[:, :, back], spread, ALU.mult).then_inc(a_acc if k == 0 else a_pv, 1)

            def a_gated(a):
                dve.wait_ge(a_gate, a.at(1, 1))
                dve.wait_ge(a_acc, per_offset.at(a, len(valid[a.c])))
                dve.tensor_tensor(acc[:, :, :], acc[:, :, :], gate[:, :, :], ALU.mult).then_inc(a_z, 1)

            def a_residual(a, u):
                rows_ = xa[:, u, :, :]
                dve.wait_ge(a_wo, a.at(1, 1))
                bank = ab[2][:, :].rearrange("p (n d) -> p n d", n=SB)
                dve.tensor_tensor(bank, bank, rows_, ALU.add).then_inc(a_otmp, 1)
                dve.wait_ge(a_otmp, a.at(1, 1))
                dve.tensor_tensor(rows_, bank, bout.unsqueeze(1).to_broadcast([P, SB, D]), ALU.add)\
                    .then_inc(a_x, 1)

            schedule(dve, {"f_norm": f_norm_, "f_turn": f_turn, "f_in": f_in, "f_hidden": f_hidden, "f_out": f_out,
                           "a_norm": a_norm_, "a_gate": a_gate_, "a_score": a_score,
                           "a_softmax": a_softmax, "a_pcut": a_pcut, "a_weigh": a_weigh, "a_gated": a_gated,
                           "a_residual": a_residual}, late=(0.0, 1.3, -1.7))

        @block.tensor
        def _(pe):
            def f_turn(r, bp, before):
                if before is not None:
                    pe.wait_ge(f_lo, before.at(LO, KH + 4 + bp + 1))
                pe.wait_ge(f_norm, r.at(2, bp + 1))
                for kc in range(KD):
                    for n in range(2):
                        last = pe.transpose(turn_bank(r, bp)[:, kc * ST + n * P:kc * ST + (n + 1) * P],
                                            f_hat[:, n, kc * P:(kc + 1) * P], ident[:, :])
                last.then_inc(f_turned, 1)

            pe.wait_ge(s_ident, 16)
            f_turn(FIRST, 0, None)
            f_turn(FIRST, 1, None)
            pe.wait_ge(s_summed, 1)
            pe.matmul(ab[0][0:1, 0:1], differ_sum[:, :], ones[:, :], start=True, stop=True).then_inc(s_counted, 1)
            pe.wait_ge(s_const, 16 * 5)
            pe.wait_ge(s_sel, 1)
            pe.wait_ge(s_flag, 1)
            has_lo = pe.value_load(flag[0:1, 0:1])

            def run_in(r, m, ring, general):
                if m == KH:
                    return
                if general:
                    (i,) = ring.of_step("f_in", m - m % 2)
                    pe.wait_ge(s_ring[i % ring.slots], ring.filled(r, i))
                if m == 0:
                    pe.wait_ge(f_tlo, r.at(2, 2))
                for w in range(2):
                    n = 2 * m + w
                    bank = f_bank(r, n)
                    if n in (2, 3):
                        after(pe, f_x, r.at(OB, n - 3))
                    elif n >= 4:
                        pe.wait_ge(f_prod if w else f_silu, r.at(KH, m - 1))
                    for k in range(KD):
                        pe.matmul(bank[:, :], w12(m, w, k), fT_hi[:, k, :], start=(k == 0), stop=False)
                        last = pe.matmul(bank[:, :], w12(m, w, k), fT_lo[:, k, :], start=False,
                                         stop=(not general and k == KD - 1))
                    for k in range(KD if general else 0):
                        o = ((m % 2) * 4 + w * 2 + k) * P
                        last = pe.matmul(bank[:, :], wring[:, i % ring.slots, o:o + P], fT_hi[:, k, :],
                                         start=False, stop=(k == KD - 1))
                    last.then_inc(f_mm, 1)

            def run_hidden(r, layer, m, ring, general):
                src = (r.p + layer) % 2
                bank = f_bank(r, hidden_use(layer, m))
                blocks = ring.of_step("f_hidden", layer, m)
                if m >= 4:
                    pe.wait_ge(f_lo, r.at(LO, (1 + layer) * KH + m - 3))
                elif layer == 0:
                    pe.wait_ge(f_prod if m % 2 else f_silu, r.at(KH, KH - 2 + m // 2 + 1))
                elif m < 2:
                    pe.wait_ge(f_lo, r.at(LO, 2 * KH - 2 + m + 1))
                elif not r.last:
                    pe.wait_ge(f_tlo, r.at(2, 2 + m - 1))
                for i in blocks:
                    pe.wait_ge(s_ring[i % ring.slots], ring.filled(r, i))
                for k in range(KH):
                    if m == 0:
                        pe.wait_ge(f_lo, r.at(LO, layer * KH + k + 1))
                    hi = wring[:, blocks[0] % ring.slots, k * P:(k + 1) * P]
                    pe.matmul(bank[:, :], hi, h_hi[src][:, k, :], start=(k == 0), stop=False)
                    last = pe.matmul(bank[:, :], hi, h_lo[src][:, k, :], start=False,
                                     stop=(not general and k == KH - 1))
                for k in range(KH if general else 0):
                    lo = wring[:, blocks[1] % ring.slots, k * P:(k + 1) * P]
                    last = pe.matmul(bank[:, :], lo, h_hi[src][:, k, :], start=False, stop=(k == KH - 1))
                last.then_inc(f_mm, 1)

            def run_out(r, ring, general):
                blocks = ring.of_step("f_out")
                for i in blocks:
                    pe.wait_ge(s_ring[i % ring.slots], ring.filled(r, i))

                def part(n, k):
                    to = out_bank(r, n // 2)[:, (n % 2) * D:(n % 2 + 1) * D]
                    t = slice(n * P, (n + 1) * P)
                    w = w_out3[:, k // 4, (k % 4) * D:(k % 4 + 1) * D]
                    pe.matmul(to, h_hi[r.p][:, k, t], w, start=(k == 0), stop=False)
                    last = pe.matmul(to, h_lo[r.p][:, k, t], w, start=False, stop=(not general and k == KH - 1))
                    if general:
                        w_lo = wring[:, blocks[k // 4] % ring.slots, (k % 4) * D:(k % 4 + 1) * D]
                        last = pe.matmul(to, h_hi[r.p][:, k, t], w_lo, start=False, stop=(k == KH - 1))
                    return last

                for b in range(OB):
                    pe.wait_ge(f_lo, r.at(LO, LO - 3 + b))
                    for k in range(KH - 1):
                        if b == 0 and k > 4:
                            pe.wait_ge(f_lo, r.at(LO, LO - KH + k + 1))
                        part(2 * b, k)
                pe.wait_ge(f_lo, r.at(LO, LO))
                for b in range(OB):
                    part(2 * b, KH - 1)
                    for k in range(KH):
                        last = part(2 * b + 1, k)
                    last.then_inc(f_mm, 1)

            def a_turn(a):
                pe.wait_ge(a_norm, a.at(1, 1))
                for kc in range(KD):
                    for n in range(SB):
                        last = pe.transpose(ab[0][:, kc * ST + n * P:kc * ST + (n + 1) * P],
                                            a_hat[:, n, kc * P:(kc + 1) * P], ident[:, :])
                last.then_inc(a_turned, 1)

            def a_project(a):
                pe.wait_ge(a_xT, a.at(1, 1))
                for w in range(4):
                    if w == 1:
                        after(pe, a_x, a.at(1, 0))
                    bank = ab[(1, 2, 3, 0)[w]]
                    for e in range(2):
                        for k in range(KD):
                            last = pe.matmul(bank[:, e * ST:(e + 1) * ST],
                                             wproj[:, k, w * D + e * P:w * D + (e + 1) * P], aT[:, k, :],
                                             start=(k == 0), stop=(k == KD - 1))
                    last.then_inc(a_proj, 1)

            def a_sum_heads(a, k):
                j = valid[a.c][k]
                g, jl = j // 8, j % 8
                v = valid[a.c]
                final = k + 1 == len(v) or v[k + 1] // 8 != g
                lo = 0 if jl == 0 else max(0, UNIQUE[j] - ST * a.c)
                rows_ = P if g < 2 else len(GROUPS[g]) * HEADS
                bank = ab[1 + g // 2]
                o = (7 - jl) * HEADS
                pe.wait_ge(a_fold, per_offset.at(a, k + 1))
                pe.matmul(bank[0:rows_, (g % 2) * ST + lo:(g % 2 + 1) * ST], sel_in[:, o:o + rows_],
                          fold[:, k % RING, lo:ST], start=(jl == 0), stop=final).then_inc(a_scored, 1)

            def a_sturn(a):
                gs = groups_of[a.c]
                pe.wait_ge(a_scopied, per_half.at(a, 2 if len(gs) > 2 else 1))
                for n in range(SB):
                    bank = ab[3] if n == 0 else ab[0]
                    for g in gs:
                        rows_ = P if g < 2 else 64
                        last = pe.transpose(bank[:, g * P:g * P + rows_], sT[0:rows_, g, n * P:(n + 1) * P],
                                            ident[0:rows_, 0:rows_])
                    last.then_inc(a_sturned, 1)

            def a_pturn(a):
                gs = groups_of[a.c]
                pe.wait_ge(a_probs, a.at(1, 1))
                for n in range(SB):
                    for g in range(2):
                        last = pe.transpose(ab[1][:, g * ST + n * P:g * ST + (n + 1) * P],
                                            S[:, n, g * P:(g + 1) * P], ident[:, :])
                last.then_inc(a_pturned, 1)
                if len(gs) > 2:
                    for n in range(SB):
                        last = pe.transpose(ab[2][0:64, n * P:(n + 1) * P], S[:, n, 2 * P:2 * P + 64], ident[:, :])
                    last.then_inc(a_pturned, 1)

            def a_spread(a, pair):
                v = valid[a.c]
                bank = ab[(3, 0, 1)[pair % 3]]
                if pair == 0:
                    pe.wait_ge(a_plo, per_half.at(a, 2 if len(groups_of[a.c]) > 2 else 1))
                if pair >= 3:
                    pe.wait_ge(a_pv, per_later_offset.at(a, 2 * (pair - 3) + 1))
                for k in range(2 * pair, min(2 * pair + 2, len(v))):
                    g, jl = v[k] // 8, v[k] % 8
                    rows_ = P if g < 2 else 64
                    to = bank[:, (k % 2) * ST:(k % 2 + 1) * ST]
                    pe.matmul(to, sel_out[0:rows_, jl, :], p_hi[0:rows_, g, :], start=True, stop=False)
                    last = pe.matmul(to, sel_out[0:rows_, jl, :], p_lo[0:rows_, g, :], start=False, stop=True)
                last.then_inc(a_spread_done, 1)

            def a_wout(a):
                pe.wait_ge(a_z, a.at(1, 1))
                for n in range(SB):
                    for e in range(2):
                        last = pe.matmul(ab[2][:, n * D:(n + 1) * D], acc[:, e, n * P:(n + 1) * P], wo[:, e, :],
                                         start=(e == 0), stop=(e == 1))
                last.then_inc(a_wo, 1)

            def run(general):
                ring = Ring(general)
                schedule(pe, {
                    "f_turn": f_turn,
                    "f_in": lambda r, m: run_in(r, m, ring, general),
                    "f_hidden": lambda r, layer, m: run_hidden(r, layer, m, ring, general),
                    "f_out": lambda r: run_out(r, ring, general),
                    "a_turn": a_turn, "a_project": a_project, "a_sum_heads": a_sum_heads, "a_sturn": a_sturn,
                    "a_pturn": a_pturn, "a_spread": a_spread, "a_wout": a_wout,
                }, at="start")

            with pe.If(has_lo != 0):
                run(True)
            with pe.Else():
                run(False)


def _lay_out(inputs):
    import numpy as np
    g = {k: np.asarray(v) for k, v in inputs.items()}
    P, heads, dh, d, hid = 128, 16, 16, 256, 1024
    kh, kd = hid // P, d // P
    blocks = []
    for n in ("h1", "h2"):
        w = g[f"L0_ffn_{n}_w"].reshape(kh, P, kh, P)
        blocks.append(w.transpose(0, 3, 2, 1).reshape(kh, P, kh * P))
    w12 = np.stack([g["L0_ffn_w1_w"], g["L0_ffn_w2_w"]]).reshape(2, kh // 2, 2, P, kd, P)
    blocks.append(w12.transpose(1, 5, 2, 0, 4, 3).reshape(kh // 2, P, 8 * P))
    w3 = g["L0_ffn_w3_w"].reshape(d, 2, 4, P)
    blocks.append(w3.transpose(1, 3, 2, 0).reshape(2, P, 4 * d))
    ffn_w = np.concatenate(blocks)

    def split_heads(a, axis):
        s = a.shape
        a = a.reshape(s[:axis] + (-1, heads, 2, dh // 2) + s[axis + 1:])
        return np.moveaxis(a, axis + 2, axis + 1).reshape(s)

    proj = np.concatenate([split_heads(g["L0_attn_Wqkv"], 1), split_heads(g["L0_attn_Wgate"], 1)], axis=1)
    proj_w = proj.reshape(kd, P, 4 * d).transpose(1, 0, 2)
    out_w = split_heads(g["L0_attn_Wout"], 0).reshape(2, P, d).transpose(1, 0, 2)
    scales = [g[f"L0_ffn_{n}_s"].reshape(kh, P) for n in ("w1", "w2", "h1", "h2")]
    cols = np.concatenate(scales + [split_heads(g["L0_attn_bqkv"], 0).reshape(6, P),
                                    split_heads(g["L0_attn_bgate"], 0).reshape(2, P)]).T
    first = [OFFSETS.index(o) for o in UNIQUE]
    second = [len(OFFSETS) - 1 - OFFSETS[::-1].index(o) for o in TWICE]
    rows = np.concatenate([g["L0_ffn_w3_s"], g["L0_attn_bout"], g["L0_attn_pos_bias"][first + second].reshape(-1)])
    masks = np.zeros((P, P + 15 * heads + 8 * P), np.float32)
    p = np.arange(P)
    masks[p, p] = 1.0
    masks[p, P + 7 * heads + p // 8] = 1.0
    for j in range(8):
        f = np.arange(P)
        masks[heads * j + f // 8, P + 15 * heads + j * P + f] = 1.0
    return {"x": g["L0_attn_x"], "ffn_w": ffn_w, "proj_w": proj_w, "out_w": out_w, "cols": cols,
            "rows": rows, "masks": masks}


def kernel(**inputs):
    import numpy as np
    import concourse.bacc as bacc
    from concourse.bass_utils import run_bass_kernel_spmd

    nc = bacc.Bacc("TRN2", target_bir_lowering=False, num_devices=1)
    arrays, args = {}, []
    for name, a in _lay_out(inputs).items():
        a = np.ascontiguousarray(a)
        arrays[f"in_{name}"] = a
        args.append(nc.dram_tensor(f"in_{name}", a.shape, mybir.dt.from_np(a.dtype), kind="ExternalInput").ap())
    shape = arrays["in_x"].shape
    args.append(nc.dram_tensor("out_x", shape, mybir.dt.float32, kind="ExternalOutput").ap())
    macaron_kernel(nc, *args)
    r = run_bass_kernel_spmd(nc, [arrays], core_ids=[0])
    return r.results[0]["out_x"]
```
